# Optimizing a Trainium2 kernel written in Bass

```python
import numpy as np
import jax
import jax.numpy as jnp

def _softmax(x, axis=-1):
    return jax.nn.softmax(x, axis=axis)

def _gelu(x):
    return jax.nn.gelu(x, approximate=True)

def _silu(x):
    return jax.nn.silu(x)

def _sigmoid(x):
    return jax.nn.sigmoid(x)

def _layernorm(x, axis=-1, eps=1e-05):
    m = jnp.mean(x, axis=axis, keepdims=True)
    v = jnp.var(x, axis=axis, keepdims=True)
    return (x - m) / jnp.sqrt(v + eps)

def _scatter_add(tgt, idx, src, axis=0):
    return tgt.at[idx].add(src)

def _segment_sum(src, seg, n):
    return jax.ops.segment_sum(src, seg, n)
kernel_name = 'mk_sandwich_d1_jaxref_r8_e312d3'

def setup_inputs(seed: int=0):
    np.random.seed(seed)
    _w = jnp.asarray

    def _L0_attn_setup():
        import jax, jax.numpy as jnp
        import numpy as np
        EPS_FEAT = 1.0 + 0.0001
        EPS_DEN = 1e-06

        def _linear_attention(x, W_qkv, b_qkv, W_out, b_out, num_heads=16):
            B, L, D = x.shape
            H = num_heads
            E = D // H
            qkv = x @ W_qkv + b_qkv
            q, k, v = jnp.split(qkv, 3, axis=-1)
            q = q.reshape(B, L, H, E)
            k = k.reshape(B, L, H, E)
            v = v.reshape(B, L, H, E)
            q = jax.nn.elu(q * E ** (-0.5)) + EPS_FEAT
            k = jax.nn.elu(k) + EPS_FEAT
            qL = jnp.moveaxis(q, 1, 0)
            kL = jnp.moveaxis(k, 1, 0)
            vL = jnp.moveaxis(v, 1, 0)
            kv0 = jnp.zeros((B, H, E, E), dtype=x.dtype)
            ks0 = jnp.zeros((B, H, E), dtype=x.dtype)

            def step(carry, qkv_t):
                kv_s, k_s = carry
                q_t, k_t, v_t = qkv_t
                kv_s = kv_s + jnp.einsum('bhe,bhf->bhef', k_t, v_t)
                k_s = k_s + k_t
                num = jnp.einsum('bhe,bhef->bhf', q_t, kv_s)
                den = jnp.einsum('bhe,bhe->bh', q_t, k_s)[..., None] + EPS_DEN
                return ((kv_s, k_s), num / den)
            _, out = jax.lax.scan(step, (kv0, ks0), (qL, kL, vL))
            out = jnp.moveaxis(out, 0, 1).reshape(B, L, D)
            return out @ W_out + b_out
        key = jax.random.key(seed)
        k1, k2, k3 = jax.random.split(key, 3)
        B, L, D = (4, 512, 128)
        x = jax.random.normal(k1, (B, L, D), dtype=jnp.float32)
        W_qkv = jax.random.normal(k2, (D, 3 * D), dtype=jnp.float32) / np.sqrt(D)
        b_qkv = jnp.zeros((3 * D,), dtype=jnp.float32)
        W_out = jax.random.normal(k3, (D, D), dtype=jnp.float32) / np.sqrt(D)
        b_out = jnp.zeros((D,), dtype=jnp.float32)
        return {'x': x, 'W_qkv': W_qkv, 'b_qkv': b_qkv, 'W_out': W_out, 'b_out': b_out}
    _L0_attn_in = _L0_attn_setup()

    def _L0_ffn_setup():
        import jax, jax.numpy as jnp
        import numpy as np
        import math
        N_EMBD = 128
        HIDDEN = 4 * N_EMBD
        N_EXPERTS = 8
        TOP_K = 2
        B, T = (4, 256)

        def new_gelu(x):
            c = math.sqrt(2.0 / math.pi)
            return 0.5 * x * (1.0 + jnp.tanh(c * (x + 0.044715 * x * x * x)))

        def _moe_forward(x, Wfc_s, bfc_s, Wproj_s, bproj_s, Wr, Wfc, bfc, Wproj, bproj):
            Bb, Tt, C = x.shape
            xf = x.reshape(Bb * Tt, C)
            N = Bb * Tt
            shared = new_gelu(xf @ Wfc_s + bfc_s) @ Wproj_s + bproj_s
            logits = xf @ Wr
            probs = jax.nn.softmax(logits, axis=-1)
            topk_p, topk_i = jax.lax.top_k(probs, TOP_K)
            topk_p = topk_p / jnp.sum(topk_p, axis=-1, keepdims=True)
            gate = jnp.zeros((N, N_EXPERTS), dtype=xf.dtype)
            gate = gate.at[jnp.arange(N)[:, None], topk_i].add(topk_p)
            routed = jnp.zeros_like(xf)
            for e in range(N_EXPERTS):
                h = new_gelu(xf @ Wfc[e] + bfc[e]) @ Wproj[e] + bproj[e]
                routed = routed + h * gate[:, e:e + 1]
            return (shared + routed).reshape(Bb, Tt, C)
        key = jax.random.key(seed)
        ks = jax.random.split(key, 10)
        s = 0.02
        return {'x': jax.random.normal(ks[0], (B, T, N_EMBD), dtype=jnp.float32), 'Wfc_s': jax.random.normal(ks[1], (N_EMBD, HIDDEN), dtype=jnp.float32) * s, 'bfc_s': jnp.zeros((HIDDEN,), dtype=jnp.float32), 'Wproj_s': jax.random.normal(ks[2], (HIDDEN, N_EMBD), dtype=jnp.float32) * s, 'bproj_s': jnp.zeros((N_EMBD,), dtype=jnp.float32), 'Wr': jax.random.normal(ks[3], (N_EMBD, N_EXPERTS), dtype=jnp.float32) * s, 'Wfc': jax.random.normal(ks[4], (N_EXPERTS, N_EMBD, HIDDEN), dtype=jnp.float32) * s, 'bfc': jnp.zeros((N_EXPERTS, HIDDEN), dtype=jnp.float32), 'Wproj': jax.random.normal(ks[5], (N_EXPERTS, HIDDEN, N_EMBD), dtype=jnp.float32) * s, 'bproj': jnp.zeros((N_EXPERTS, N_EMBD), dtype=jnp.float32)}
    _L0_ffn_in = _L0_ffn_setup()
    _d = {'L0_attn_x': _L0_attn_in['x'], 'L0_attn_W_qkv': _L0_attn_in['W_qkv'], 'L0_attn_b_qkv': _L0_attn_in['b_qkv'], 'L0_attn_W_out': _L0_attn_in['W_out'], 'L0_attn_b_out': _L0_attn_in['b_out'], 'L0_ffn_Wfc_s': _L0_ffn_in['Wfc_s'], 'L0_ffn_bfc_s': _L0_ffn_in['bfc_s'], 'L0_ffn_Wproj_s': _L0_ffn_in['Wproj_s'], 'L0_ffn_bproj_s': _L0_ffn_in['bproj_s'], 'L0_ffn_Wr': _L0_ffn_in['Wr'], 'L0_ffn_Wfc': _L0_ffn_in['Wfc'], 'L0_ffn_bfc': _L0_ffn_in['bfc'], 'L0_ffn_Wproj': _L0_ffn_in['Wproj'], 'L0_ffn_bproj': _L0_ffn_in['bproj']}
    _x0 = _d['L0_attn_x']
    _d['L0_attn_x'] = jax.random.normal(jax.random.fold_in(jax.random.key(seed), 1), (16, 256, 128), dtype=_x0.dtype)
    del _x0
    return _d

def reference(L0_attn_x, L0_attn_W_qkv, L0_attn_b_qkv, L0_attn_W_out, L0_attn_b_out, L0_ffn_Wfc_s, L0_ffn_bfc_s, L0_ffn_Wproj_s, L0_ffn_bproj_s, L0_ffn_Wr, L0_ffn_Wfc, L0_ffn_bfc, L0_ffn_Wproj, L0_ffn_bproj):

    def _L0_attn_ref(x, W_qkv, b_qkv, W_out, b_out):
        import jax, jax.numpy as jnp
        import numpy as np
        EPS_FEAT = 1.0 + 0.0001
        EPS_DEN = 1e-06

        def _linear_attention(x, W_qkv, b_qkv, W_out, b_out, num_heads=16):
            B, L, D = x.shape
            H = num_heads
            E = D // H
            qkv = x @ W_qkv + b_qkv
            q, k, v = jnp.split(qkv, 3, axis=-1)
            q = q.reshape(B, L, H, E)
            k = k.reshape(B, L, H, E)
            v = v.reshape(B, L, H, E)
            q = jax.nn.elu(q * E ** (-0.5)) + EPS_FEAT
            k = jax.nn.elu(k) + EPS_FEAT
            qL = jnp.moveaxis(q, 1, 0)
            kL = jnp.moveaxis(k, 1, 0)
            vL = jnp.moveaxis(v, 1, 0)
            kv0 = jnp.zeros((B, H, E, E), dtype=x.dtype)
            ks0 = jnp.zeros((B, H, E), dtype=x.dtype)

            def step(carry, qkv_t):
                kv_s, k_s = carry
                q_t, k_t, v_t = qkv_t
                kv_s = kv_s + jnp.einsum('bhe,bhf->bhef', k_t, v_t)
                k_s = k_s + k_t
                num = jnp.einsum('bhe,bhef->bhf', q_t, kv_s)
                den = jnp.einsum('bhe,bhe->bh', q_t, k_s)[..., None] + EPS_DEN
                return ((kv_s, k_s), num / den)
            _, out = jax.lax.scan(step, (kv0, ks0), (qL, kL, vL))
            out = jnp.moveaxis(out, 0, 1).reshape(B, L, D)
            return out @ W_out + b_out
        return _linear_attention(x, W_qkv, b_qkv, W_out, b_out)

    def _L0_ffn_ref(x, Wfc_s, bfc_s, Wproj_s, bproj_s, Wr, Wfc, bfc, Wproj, bproj):
        import jax, jax.numpy as jnp
        import numpy as np
        import math
        N_EMBD = 128
        HIDDEN = 4 * N_EMBD
        N_EXPERTS = 8
        TOP_K = 2
        B, T = (4, 256)

        def new_gelu(x):
            c = math.sqrt(2.0 / math.pi)
            return 0.5 * x * (1.0 + jnp.tanh(c * (x + 0.044715 * x * x * x)))

        def _moe_forward(x, Wfc_s, bfc_s, Wproj_s, bproj_s, Wr, Wfc, bfc, Wproj, bproj):
            Bb, Tt, C = x.shape
            xf = x.reshape(Bb * Tt, C)
            N = Bb * Tt
            shared = new_gelu(xf @ Wfc_s + bfc_s) @ Wproj_s + bproj_s
            logits = xf @ Wr
            probs = jax.nn.softmax(logits, axis=-1)
            topk_p, topk_i = jax.lax.top_k(probs, TOP_K)
            topk_p = topk_p / jnp.sum(topk_p, axis=-1, keepdims=True)
            gate = jnp.zeros((N, N_EXPERTS), dtype=xf.dtype)
            gate = gate.at[jnp.arange(N)[:, None], topk_i].add(topk_p)
            routed = jnp.zeros_like(xf)
            for e in range(N_EXPERTS):
                h = new_gelu(xf @ Wfc[e] + bfc[e]) @ Wproj[e] + bproj[e]
                routed = routed + h * gate[:, e:e + 1]
            return (shared + routed).reshape(Bb, Tt, C)
        return _moe_forward(x, Wfc_s, bfc_s, Wproj_s, bproj_s, Wr, Wfc, bfc, Wproj, bproj)
    x = L0_attn_x
    x = x + _layernorm(_L0_attn_ref(_layernorm(x, axis=-1), L0_attn_W_qkv, L0_attn_b_qkv, L0_attn_W_out, L0_attn_b_out), axis=-1)
    x = x + _layernorm(_L0_ffn_ref(_layernorm(x, axis=-1), L0_ffn_Wfc_s, L0_ffn_bfc_s, L0_ffn_Wproj_s, L0_ffn_bproj_s, L0_ffn_Wr, L0_ffn_Wfc, L0_ffn_bfc, L0_ffn_Wproj, L0_ffn_bproj), axis=-1)
    return x

_drawn_inputs = setup_inputs


def setup_inputs(seed=0):
    import zlib

    import numpy as np

    out = dict(_drawn_inputs(seed))
    spreads = {'L0_attn_b_qkv': (0.0, 0.1),
     'L0_attn_b_out': (0.0, 0.1),
     'L0_ffn_bfc_s': (0.0, 0.1),
     'L0_ffn_bproj_s': (0.0, 0.1),
     'L0_ffn_bfc': (0.0, 0.1),
     'L0_ffn_bproj': (0.0, 0.1)}
    factors = {}
    for name, (base, spread) in spreads.items():
        noise = np.random.default_rng([zlib.crc32(name.encode()), seed]).standard_normal(out[name].shape)
        drawn = base * np.exp(spread * noise) if base else spread * noise
        out[name] = jnp.asarray(drawn.astype(out[name].dtype))
    for name, factor in factors.items():
        out[name] = (out[name] * factor).astype(out[name].dtype)
    return out
```

```python
from contextlib import ExitStack

import concourse.bass as bass
from concourse import mybir

ALU = mybir.AluOpType
ACT = mybir.ActivationFunctionType
F32 = mybir.dt.float32
BF16 = mybir.dt.bfloat16
I32 = mybir.dt.int32
U32 = mybir.dt.uint32
AX_X = mybir.AxisListType.X

P = 128
D = 128
H, E = 16, 8
L = 256
TILES = 4
STEP = TILES * P
HID = 512
CH = HID // P
NE = 8
BLK = 256
FEAT_EPS = 1e-4
DEN_EPS = 1e-6
LN_EPS = 1e-5


def sandwich_kernel(nc, x, w_qkv, b_qkv, w_out, b_out, wfc_s, bfc_s, wproj_s, bproj_s, wr, wfc, bfc, wproj,
                    bproj, out):
    x_rows = x.rearrange("b l d -> (b l) d")
    out_rows = out.rearrange("b l d -> (b l) d")
    TOKENS = x_rows.shape[0]
    NS = TOKENS // STEP
    NT = TOKENS // P
    PAIRS = 2 * TOKENS
    NB = PAIRS // BLK + NE - 1
    SPARE = NB - PAIRS // BLK
    LIST = TOKENS + BLK
    ROW = D + 1
    WROW = HID + CH * D + CH + D
    B1_AT = HID + CH * D
    B2_AT = B1_AT + CH
    PADS = NE + SPARE
    NBUF = 3
    NFIN = 3
    assert NB % NBUF == 0

    lists = nc.dram_tensor("expert_lists", [NE * LIST + SPARE * BLK, ROW], F32).ap()
    results = nc.dram_tensor("expert_results", [PAIRS + PADS * BLK, D], F32).ap()
    packed = nc.dram_tensor("packed_weights", [NE, P, WROW], F32).ap()

    with ExitStack() as ctx:
        def sb(name, shape, dt=F32):
            return ctx.enter_context(nc.sbuf_tensor(name, shape, dt))

        def bank(name, shape, dt=F32):
            return ctx.enter_context(nc.psum_tensor(name, shape, dt))

        def sem(name):
            return ctx.enter_context(nc.semaphore(name))

        ident = sb("ident", [P, P])
        row0 = sb("row0", [P, P])
        head_ones = sb("head_ones", [P, H])
        before = sb("before", [P, P], BF16)
        ones_bf = sb("ones_bf", [P, P], BF16)
        keep = sb("keep", [P, 2 * STEP], BF16)
        iota8 = sb("iota8", [P, NE])
        list_base = sb("list_base", [P, NE])
        dest = sb("dest", [P, NS, 2, TILES], I32)
        neg_half = sb("neg_half", [P, TILES])
        ln_eps = sb("ln_eps", [P, TILES])
        wqkv_raw = sb("wqkv_raw", [P, 3 * D])
        wqkv_sb = sb("wqkv_sb", [P, 3, E, H])
        wout_sb = sb("wout_sb", [P, D])
        wout_t = sb("wout_t", [P, 2, E, H])
        wout_rot = sb("wout_rot", [P, E, D])
        wr_sb = sb("wr_sb", [P, NE])
        w1s_sb = sb("w1s_sb", [P, HID])
        w2s_sb = sb("w2s_sb", [P, CH, D])
        NBIAS = NE * CH + CH
        bias_rows = sb("bias_rows", [NBIAS, P])
        bias_cols = sb("bias_cols", [P, NBIAS])
        bqkv_raw = sb("bqkv_raw", [3, D])
        bqkv_rows = sb("bqkv_rows", [3, E, H])
        bq_scaled = sb("bq_scaled", [P, 1])
        bk_col = sb("bk_col", [P, 1])
        bv_raw = sb("bv_raw", [1, D])
        bv_mat = sb("bv_mat", [P, TILES, D])
        bo_mat = sb("bo_mat", [P, TILES, D])
        b2s_mat = sb("b2s_mat", [P, TILES, D])
        b12 = sb("b12", [P, NE, CH + D])
        pads = sb("pads", [P, PADS, 2, ROW])
        X = sb("X", [P, NT, D])
        SH = sb("SH", [P, NT, D])
        bst = sb("bst", [P, 3, TILES, 6])
        mv = sb("mv", [P, 3, TILES, 2])
        ve = sb("ve", [P, 3, TILES])
        rstd = sb("rstd", [P, 3, TILES])
        xn = sb("xn", [P, TILES, D])
        xn_t = sb("xn_t", [P, STEP])
        e_qk = sb("e_qk", [P, 2, STEP])
        r_qk = sb("r_qk", [P, 2, STEP])
        qk0 = sb("qk0", [P, 2, STEP])
        k1 = sb("k1", [P, STEP])
        vdup = sb("vdup", [P, TILES, 2 * D])
        KV = sb("KV", [P, E, STEP])
        KC = sb("KC", [P, STEP])
        pden = sb("pden", [P, STEP])
        den = sb("den", [P, TILES * H])
        rden = sb("rden", [P, TILES, H])
        rden8 = sb("rden8", [P, TILES, E, H])
        qn = sb("qn", [P, STEP])
        Z = sb("Z", [P, E, STEP])
        attn = sb("attn", [P, TILES, D])
        rows = sb("rows", [P, 2, TILES, ROW])
        xt2 = sb("xt2", [P, STEP])
        hs = sb("hs", [P, CH, STEP])
        lg = sb("lg", [P, TILES, NE])
        top = sb("top", [P, TILES, 8])
        topi = sb("topi", [P, TILES, 8], U32)
        idxf = sb("idxf", [P, 2, TILES])
        onehot = sb("onehot", [P, 2, TILES, NE])
        chosen = sb("chosen", [P, TILES, NE], BF16)
        chosen_sum = sb("chosen_sum", [P, NE])
        chosen_acc = sb("chosen_acc", [P, NE], BF16)
        gap = sb("gap", [P, NT])
        place = sb("place", [P, TILES, NE])
        placed = sb("placed", [P, 2, TILES, NE])
        posf = sb("posf", [P, 2 * TILES])
        pos = sb("pos", [P, 2 * TILES], I32)
        gates = sb("gates", [P, 2, NT])
        cnt = sb("cnt", [1, NE])
        steps16 = sb("steps16", [1, NE, LIST // BLK - 1])
        full16 = sb("full16", [1, NE, LIST // BLK - 1])
        nblk = sb("nblk", [1, NE])
        cum = sb("cum", [1, NE])
        one8 = sb("one8", [1, NE])
        jump = sb("jump", [1, NE])
        bnum = sb("bnum", [1, NB, NE])
        past = sb("past", [1, NB, NE])
        pastj = sb("pastj", [1, NB, NE])
        b256 = sb("b256", [1, NB])
        tabf = sb("tabf", [1, 3 * NB])
        table = sb("table", [1, 2 * NB + NE], I32)
        wb = [sb(f"wb{n}", [P, WROW]) for n in range(NBUF)]
        xb = [sb(f"xb{n}", [P, 2, ROW]) for n in range(NBUF)]
        xbt = [sb(f"xbt{n}", [P, BLK]) for n in range(NBUF)]
        hb = [sb(f"hb{n}", [P, CH, BLK]) for n in range(NBUF)]
        yb = [sb(f"yb{n}", [P, 2, D]) for n in range(NBUF)]
        Y = Z[:].rearrange("p a t -> p (a t)")[:, 0:NFIN * TILES * 2 * D].rearrange(
            "p (n t k d) -> p n t k d", n=NFIN, t=TILES, k=2)
        fin = sb("fin", [P, NFIN, TILES, D])

        bT = bank("bT", [P, STEP])
        bA = bank("bA", [P, STEP])
        bB = bank("bB", [P, STEP])
        bV = [bank(f"bV{n}", [P, STEP]) for n in range(2)]
        bO = bank("bO", [P, STEP])
        bS = bank("bS", [P, STEP])
        bH = bank("bH", [P, STEP])
        ps_den, ps_lg, ps_rank = bS[:, 0:TILES * H], bS[:, 64:64 + TILES * NE], bS[:, 128:128 + TILES * NE]
        blk_t = [bT[:, 0:BLK], bH[:, 0:BLK]]
        blk_h = [[bA, bB], [bV[0], bV[1]]]
        blk_y = [bO, bS]

        names = """waited x_first x_rest w_first w_rest bias_in bo_in b2s_in b2_in packed_w packed_b
            consts setup_pe setup_dve
            ln0_mv ln0_rstd xn_ready t0_done xnt_ready q_mm k_mm v_mm q_read qk_read vdup_ready qk_ready k1_ready
            vt_done kv_prod kc_ready kv_sum p_ready den_done den_add den_inv rden_ready exp_done qn_ready z_ready out_done
            ln1_st ln1_mv ln1_rstd attn_ready x1_ready ln2_st ln2_mv ln2_rstd ln0_st ve_ready
            xn2_ready dest_ready rows_ready t2_done xt2_ready
            fc_done gelu_done sh_done sh_read
            lg_done lg_read top_ready idx_ready hot_ready hot_both chosen_ready rank_done acc_red acc_ready
            place_ready placed_ready posf_ready pos_ready scattered
            pads_ready spare_in cnt_done tab table_ready tails_in
            blk_tp blk_tr blk_fc blk_gelu blk_mm2 blk_yr
            gate_exp gate_w fin_y0 fin_y1 fin_st fin_mv fin_ve fin_rstd fin_n fin_done""".split()
        s = {n: sem(n) for n in names}
        wb_in = [sem(f"wb_in{n}") for n in range(NBUF)]
        xb_in = [sem(f"xb_in{n}") for n in range(NBUF)]
        blk_scat = [sem(f"blk_scat{n}") for n in range(NBUF)]
        y_in = [sem(f"y_in{n}") for n in range(NS)]
        out_stored = [sem(f"out_stored{n}") for n in range(NS)]
        block = ctx.enter_context(nc.Block())

        def alone(eng):
            eng.sem_inc(s["waited"], 1)

        def block_loop(eng, body, reuse, wait_reuse):
            def one(b, n, again):
                if again and wait_reuse:
                    eng.wait_ge(s[reuse], b - NBUF + 1)
                body(b, n % NBUF, n % 2)

            span = 2 * NBUF
            for n in range(NBUF):
                one(n, n, False)
            rest = NB - NBUF
            with eng.Fori(0, rest // span) as it:
                for n in range(span):
                    one(it * span + NBUF + n, NBUF + n, True)
            for n in range(rest - rest % span + NBUF, NB):
                one(n, n, True)

        def store(sp, g):
            sp.wait_ge(s["fin_done"], g + 1)
            sp.dma_start(out_rows[g * STEP:(g + 1) * STEP, :].rearrange("(t p) d -> p t d", p=P),
                         fin[:, g % NFIN]).then_inc(out_stored[g], 16)

        @block.sync
        def _(sp):
            def xt(a, b):
                return x_rows[a * P:b * P, :].rearrange("(t p) d -> p t d", p=P)

            sp.dma_start(X[:, 0:TILES, :], xt(0, TILES)).then_inc(s["x_first"], 16)
            sp.dma_start(wqkv_raw[:], w_qkv).then_inc(s["w_first"], 16)
            sp.dma_start(wout_sb[:], w_out).then_inc(s["w_first"], 16)
            n = NE * CH
            sp.dma_start(bias_rows[0:n, :], bfc.rearrange("e (c p) -> (e c) p", p=P)).then_inc(s["bias_in"], 16)
            sp.dma_start(bias_rows[n:n + CH, :], bfc_s.rearrange("(c p) -> c p", p=P)).then_inc(s["bias_in"], 16)
            sp.dma_start(bqkv_raw[:], b_qkv.rearrange("(c p) -> c p", p=P)).then_inc(s["bias_in"], 16)
            sp.dma_start(bv_raw[:], b_qkv[2 * D:3 * D].rearrange("(o d) -> o d", o=1)).then_inc(s["bias_in"], 16)
            sp.wait_ge(s["consts"], 1)
            for mat, src, done in ((bo_mat, b_out, "bo_in"), (b2s_mat, bproj_s, "b2s_in")):
                for j in range(TILES):
                    sp.dma_start(mat[0:1, j, :], src.rearrange("(o d) -> o d", o=1)).then_inc(s[done], 16)
            sp.dma_start(X[:, TILES:NT, :], xt(TILES, NT)).then_inc(s["x_rest"], 16)
            sp.dma_start(wr_sb[:], wr).then_inc(s["w_rest"], 16)
            sp.dma_start(w1s_sb[:], wfc_s).then_inc(s["w_rest"], 16)
            sp.dma_start(w2s_sb[:], wproj_s.rearrange("(c p) n -> p c n", p=P)).then_inc(s["w_rest"], 16)
            sp.dma_start(b12[:, :, CH:CH + D], bproj.rearrange("(o e) d -> o e d", o=1).broadcast_to([P, NE, D])
                         ).then_inc(s["b2_in"], 16)
            for e in range(NE):
                sp.dma_start(packed[e, :, 0:HID], wfc[e]).then_inc(s["packed_w"], 16)
                sp.dma_start(packed[e, :, HID:B1_AT].rearrange("p (c n) -> p c n", c=CH),
                             wproj[e].rearrange("(c p) n -> p c n", p=P)).then_inc(s["packed_w"], 16)
            sp.wait_ge(s["b2_in"], 16)
            sp.wait_ge(s["setup_dve"], 4)
            sp.dma_start(packed[:, :, B1_AT:WROW].rearrange("e p n -> p e n"), b12[:]).then_inc(s["packed_b"], 16)
            sp.wait_ge(s["pads_ready"], 2)
            sp.dma_start(lists[NE * LIST:, :].rearrange("(c p) n -> p c n", p=P),
                         pads[:, NE:PADS, :, :].rearrange("p a c n -> p (a c) n")).then_inc(s["spare_in"], 16)
            sp.wait_ge(s["spare_in"], 16)
            sp.wait_ge(s["table_ready"], 1)
            sp.wait_ge(s["scattered"], 16 * 2 * NT)
            for e in range(NE):
                at = sp.value_load(table[0:1, 2 * NB + e:2 * NB + e + 1], min_val=e * LIST,
                                   max_val=e * LIST + TOKENS)
                sp.dma_start(lists[bass.ds(at, BLK), :].rearrange("(c p) n -> p c n", p=P),
                             pads[:, e, :, :]).then_inc(s["tails_in"], 16)
            sp.wait_ge(s["tails_in"], 16 * NE)
            sp.wait_ge(s["packed_w"], 16 * 2 * NE)
            sp.wait_ge(s["packed_b"], 16)

            def load_block(b, buf, reuse):
                who = sp.value_load(table[0:1, bass.ds(b, 1)], min_val=0, max_val=NE - 1)
                at = sp.value_load(table[0:1, bass.ds(b + NB, 1)], min_val=0,
                                   max_val=NE * LIST + (SPARE - 1) * BLK)
                if reuse is not None:
                    sp.wait_ge(blk_scat[buf], 32 * reuse)
                    alone(sp)
                    sp.wait_ge(s["blk_yr"], b - NBUF + 1)
                sp.dma_start(xb[buf][:], lists[bass.ds(at, BLK), :].rearrange("(c p) n -> p c n", p=P)
                             ).then_inc(xb_in[buf], 16)
                sp.dma_start(wb[buf][:], packed[bass.ds(who, 1), :, :].rearrange("e p n -> p (e n)")
                             ).then_inc(wb_in[buf], 16)

            for n in range(NBUF):
                load_block(n, n, None)
            with sp.Fori(1, NB // NBUF) as it:
                for n in range(NBUF):
                    load_block(it * NBUF + n, n, it)
            for n in range(NBUF):
                sp.wait_ge(blk_scat[n], 32 * (NB // NBUF))
            for g in range(NS):
                if g >= NFIN:
                    sp.wait_ge(s["fin_y1"], g - NFIN + 1)
                sp.dma_start(Y[:, g % NFIN].rearrange("p t k d -> p t (k d)"),
                             results[2 * g * STEP:2 * (g + 1) * STEP, :]
                             .rearrange("(t p k) d -> p t (k d)", p=P, k=2)).then_inc(y_in[g], 16)
                if g >= NFIN - 1:
                    store(sp, g - NFIN + 1)
            for g in range(NS - NFIN + 1, NS):
                store(sp, g)
            for g in range(NS):
                sp.wait_ge(out_stored[g], 16)

        @block.gpsimd
        def _(pool):
            g = nc.gpsimd
            for mat in (bv_mat, bo_mat, b2s_mat):
                last = g.memset(mat[:], 0.0)
            last.then_inc(s["consts"], 1)
            g.memset(row0[:], 1.0)
            g.memset(ident[:], 0.0)
            g.memset(before[:], 1.0)
            g.memset(ones_bf[:], 1.0)
            g.memset(keep[:], 1.0)
            g.memset(neg_half[:], -0.5)
            g.memset(ln_eps[:], LN_EPS)
            g.memset(chosen_acc[:], 0.0)
            g.memset(one8[:], 1.0).then_inc(s["consts"], 1)
            pool.wait_ge(s["consts"], 2)
            g.affine_select(out=row0[:], in_=row0[:], compare_op=ALU.is_equal, fill=0.0, base=0,
                            pattern=[[0, P]], channel_multiplier=1)
            g.affine_select(out=ident[:], in_=ident[:], compare_op=ALU.not_equal, fill=1.0, base=0,
                            pattern=[[-1, P]], channel_multiplier=1)
            g.affine_select(out=before[:], in_=before[:], compare_op=ALU.is_gt, fill=0.0, base=0,
                            pattern=[[1, P]], channel_multiplier=-1).then_inc(s["consts"], 1)
            g.memset(keep[:].rearrange("p (a b) -> p a b", b=L)[:, :, 0:1], 0.0)
            g.iota(iota8[:], [[1, NE]], base=0, channel_multiplier=0, allow_small_or_imprecise_dtypes=True)
            g.iota(list_base[:], [[LIST, NE]], base=0, channel_multiplier=0,
                   allow_small_or_imprecise_dtypes=True)
            g.iota(dest[:], [[2 * STEP, NS], [1, 2], [2 * P, TILES]], base=0, channel_multiplier=2)
            g.iota(steps16[:], [[0, NE], [BLK, LIST // BLK - 1]], base=0, channel_multiplier=0,
                   allow_small_or_imprecise_dtypes=True)
            g.iota(bnum[:], [[1, NB], [0, NE]], base=0, channel_multiplier=0, allow_small_or_imprecise_dtypes=True)
            g.iota(b256[:], [[BLK, NB]], base=0, channel_multiplier=0,
                   allow_small_or_imprecise_dtypes=True).then_inc(s["consts"], 1)

            def inv_std(which, st, got):
                pool.wait_ge(s[got], st + 1)
                if which == 0:
                    pool.wait_ge(s["consts"], 4)
                g.tensor_tensor(ve[:, which], mv[:, which, :, 1], ln_eps[:], ALU.add).then_inc(s["ve_ready"], 1)
                return which

            def inv_std2(which, order, name):
                pool.wait_ge(s["ve_ready"], order)
                g.tensor_tensor(rstd[:, which], ve[:, which], neg_half[:], ALU.pow).then_inc(s[name], 1)

            inv_std(0, 0, "ln0_mv")
            inv_std2(0, 1, "ln0_rstd")
            g.memset(pads[:], 0.0).then_inc(s["pads_ready"], 1)
            pool.wait_ge(s["pads_ready"], 1)
            g.iota(pads[:].bitcast(I32)[:, :, :, D:ROW], [[BLK, PADS], [P, 2], [0, 1]], base=PAIRS,
                   channel_multiplier=1).then_inc(s["pads_ready"], 1)

            def iteration(i, head, tail, nxt):
                n = 0
                base = 3 * i - 1 if head else 3 * i - 2
                if tail:
                    inv_std(1, i - 1, "ln1_mv")
                    n += 1
                    inv_std2(1, base + n, "ln1_rstd")
                    pool.wait_ge(s["attn_ready"], 4 * i)
                    Xs = X[:, bass.ds(TILES * (i - 1), TILES), :]
                    g.tensor_tensor(Xs, Xs, attn[:], ALU.add).then_inc(s["x1_ready"], 1)
                    inv_std(2, i - 1, "ln2_mv")
                    n += 1
                    inv_std2(2, base + n, "ln2_rstd")
                if nxt:
                    inv_std(0, i + 1, "ln0_mv")
                    n += 1
                    inv_std2(0, (base + n) if tail else 2, "ln0_rstd")
                if tail:
                    pool.wait_ge(s["pos_ready"], i)
                    pool.wait_ge(s["dest_ready"], i)
                    pool.wait_ge(s["xn2_ready"], 4 * i)
                    pool.wait_ge(s["rows_ready"], i)
                    alone(pool)
                    for k in range(2):
                        for j in range(TILES):
                            m = k * TILES + j
                            g.indirect_dma_start(
                                out=lists, out_offset=bass.IndirectOffsetOnAxis(ap=pos[:, m:m + 1], axis=0),
                                in_=rows[:, k, j, :], in_offset=None).then_inc(s["scattered"], 16)

            iteration(0, True, False, True)
            with pool.Fori(1, NS - 1) as i:
                iteration(i, True, True, True)
            iteration(NS - 1, True, True, False)
            iteration(NS, False, True, False)

            def scatter_block(b, buf, par):
                pool.wait_ge(s["blk_yr"], b + 1)
                alone(pool)
                for c in range(2):
                    g.indirect_dma_start(
                        out=results,
                        out_offset=bass.IndirectOffsetOnAxis(ap=xb[buf][:].bitcast(I32)[:, c, D:ROW], axis=0),
                        in_=yb[buf][:, c, :], in_offset=None).then_inc(blk_scat[buf], 16)

            with pool.Fori(0, NB // NBUF) as it:
                for n in range(NBUF):
                    scatter_block(it * NBUF + n, n, n)
            for n in range(NS):
                pool.wait_ge(s["fin_ve"], n + 1)
                g.tensor_tensor(rstd[:, n % NFIN], ve[:, n % NFIN], neg_half[:], ALU.pow
                                ).then_inc(s["fin_rstd"], 1)

        @block.scalar
        def _(act):
            a = nc.scalar

            def project(st, again):
                act.wait_ge(s["t0_done"], st + 1)
                if again:
                    act.wait_ge(s["v_mm"], st)
                a.activation(xn_t[:], bT[:], ACT.Copy).then_inc(s["xnt_ready"], 1)
                act.wait_ge(s["q_mm"], st + 1)
                if again:
                    act.wait_ge(s["qk_ready"], st)
                a.activation(e_qk[:, 0], bA[:], ACT.Exp, bias=bq_scaled[:], scale=E ** -0.5)
                a.activation(r_qk[:, 0], bA[:], ACT.Relu, bias=bq_scaled[:],
                             scale=E ** -0.5).then_inc(s["q_read"], 1)
                act.wait_ge(s["k_mm"], st + 1)
                a.activation(e_qk[:, 1], bB[:], ACT.Exp, bias=bk_col[:])
                a.activation(r_qk[:, 1], bB[:], ACT.Relu, bias=bk_col[:]).then_inc(s["qk_read"], 1)
                act.wait_ge(s["v_mm"], st + 1)
                if again:
                    act.wait_ge(s["vt_done"], E * st)
                v = bA[:].rearrange("p (t d) -> p t d", t=TILES)
                a.activation(vdup[:, :, 0:D], v, ACT.Copy)
                a.activation(vdup[:, :, D:2 * D], v, ACT.Copy).then_inc(s["vdup_ready"], 1)

            act.wait_ge(s["setup_dve"], 3)
            project(0, False)

            def gelus(st, again):
                for c in range(CH):
                    act.wait_ge(s["fc_done"], CH * st + c + 1)
                    a.activation(hs[:, c], bH[:], ACT.Gelu_apprx_tanh,
                                 bias=bias_cols[:, NE * CH + c:NE * CH + c + 1]).then_inc(s["gelu_done"], 1)
                act.wait_ge(s["sh_done"], st + 1)
                a.activation(SH[:, bass.ds(TILES * st, TILES), :], bA[:].rearrange("p (t d) -> p t d", t=TILES),
                             ACT.Copy).then_inc(s["sh_read"], 1)

            def iteration(i, head, tail, nxt, shared, first=False, shared_again=True):
                if head:
                    act.wait_ge(s["qk_ready"], i + 1)
                    if not first:
                        act.wait_ge(s["kc_ready"], i)
                    a.activation(k1[:], qk0[:, 1], ACT.Copy, bias=FEAT_EPS).then_inc(s["k1_ready"], 1)
                if shared:
                    gelus(i - 2, shared_again)
                if tail:
                    act.wait_ge(s["t2_done"], i)
                    a.activation(xt2[:], bT[:], ACT.Copy).then_inc(s["xt2_ready"], 1)
                    act.wait_ge(s["xn2_ready"], 4 * i)
                    if shared:
                        act.wait_ge(s["scattered"], 16 * 2 * TILES * (i - 1))
                    a.activation(rows[:, 1, :, 0:D], rows[:, 0, :, 0:D], ACT.Copy).then_inc(s["rows_ready"], 1)
                if nxt:
                    project(i + 1, True)

            iteration(0, True, False, True, False, first=True)
            iteration(1, True, True, True, False)
            iteration(2, True, True, True, True, shared_again=False)
            with act.Fori(3, NS - 1) as i:
                iteration(i, True, True, True, True)
            iteration(NS - 1, True, True, False, True)
            iteration(NS, False, True, False, True)
            gelus(NS - 1, True)

            def block_gelu(b, buf, par):
                act.wait_ge(s["blk_fc"], b + 1)
                for c in range(CH):
                    ins = a.activation(hb[buf][:, c], blk_h[par][c // 2][:, (c % 2) * BLK:(c % 2 + 1) * BLK],
                                       ACT.Gelu_apprx_tanh, bias=wb[buf][:, B1_AT + c:B1_AT + c + 1])
                ins.then_inc(s["blk_gelu"], 1)

            block_loop(act, block_gelu, "blk_mm2", True)

            act.wait_ge(s["top_ready"], 2 * TILES * NS)
            act.wait_ge(s["idx_ready"], NS)
            a.activation(gates[:, 1], gap[:], ACT.Exp).then_inc(s["gate_exp"], 1)

        @block.tensor
        def _(pe):
            t = nc.tensor
            pe.wait_ge(s["consts"], 4)
            pe.wait_ge(s["bias_in"], 64)
            pe.wait_ge(s["setup_dve"], 1)
            t.transpose(bS[:, 0:NBIAS], bias_rows[:], ident[0:NBIAS, 0:NBIAS])
            t.transpose(bS[:, 64:67], bqkv_rows[:].rearrange("r e h -> r (e h)"), ident[0:3, 0:3]
                        ).then_inc(s["setup_pe"], 1)
            pe.wait_ge(s["w_first"], 32)
            t.transpose(bO[:, 0:D], wout_sb[:], ident[:]).then_inc(s["setup_pe"], 1)

            def ln_transposes(src, count, wait_name, value, done):
                pe.wait_ge(s[wait_name], value)
                for j in range(TILES):
                    ins = t.transpose(bT[:, j * P:(j + 1) * P], src(j), ident[:])
                ins.then_inc(s[done], 1)

            def project(st, again):
                if again:
                    pe.wait_ge(s["xt2_ready"], st - 1) if not isinstance(st, int) or st >= 2 else None
                ln_transposes(lambda j: xn[:, j], TILES, "xn_ready", 4 * st + 4, "t0_done")
                pe.wait_ge(s["xnt_ready"], st + 1)
                if again:
                    pe.wait_ge(s["vdup_ready"], st)
                    if not isinstance(st, int) or st >= 3:
                        pe.wait_ge(s["sh_read"], st - 2)
                t.matmul(bA[:], w3[:, 0:D], xn_t[:], start=True, stop=True).then_inc(s["q_mm"], 1)
                if again:
                    pe.wait_ge(s["qn_ready"], st)
                t.matmul(bB[:], w3[:, D:2 * D], xn_t[:], start=True, stop=True).then_inc(s["k_mm"], 1)
                pe.wait_ge(s["q_read"], st + 1)
                t.matmul(bA[:], row0[:], bv_mat[:].rearrange("p t d -> p (t d)"), start=True, stop=False,
                         skip_group_check=True)
                for j in range(TILES):
                    ins = t.matmul(bA[:, j * D:(j + 1) * D], xn_t[:, j * P:(j + 1) * P], w3[:, 2 * D:3 * D],
                                   start=False, stop=True, skip_group_check=True)
                ins.then_inc(s["v_mm"], 1)

            pe.wait_ge(s["setup_dve"], 2)
            w3 = wqkv_sb[:].rearrange("p m e h -> p (m e h)")
            project(0, False)
            pe.wait_ge(s["setup_dve"], 4)
            w2t = wout_t[:].rearrange("p a e h -> p (a e h)")
            for d in range(E):
                dst = bV[d // 4][:, (d % 4) * D:(d % 4 + 1) * D]
                ins = t.transpose(dst, w2t[:, d * H:d * H + D], ident[:])
            ins.then_inc(s["setup_pe"], 1)
            pe.wait_ge(s["setup_dve"], 5)
            pe.wait_ge(s["bo_in"], 16 * TILES)

            def v_rotated(st, d, again):
                if again or d >= 2:
                    pe.wait_ge(s["kv_prod"], E * st + d - 1)
                for j in range(TILES):
                    ins = t.transpose(bV[d % 2][:, j * P:(j + 1) * P], vdup[:, j, d * H:d * H + D], ident[:])
                ins.then_inc(s["vt_done"], 1)

            def fc(st, c, again):
                if again or c >= 1:
                    pe.wait_ge(s["gelu_done"], CH * st + c)
                t.matmul(bH[:], w1s_sb[:, c * P:(c + 1) * P], xt2[:], start=True,
                         stop=True).then_inc(s["fc_done"], 1)

            def proj(st, c):
                pe.wait_ge(s["gelu_done"], CH * st + c + 1)
                for j in range(TILES):
                    ins = t.matmul(bA[:, j * D:(j + 1) * D], hs[:, c, j * P:(j + 1) * P], w2s_sb[:, c],
                                   start=False, stop=True, skip_group_check=True)
                if c == CH - 1:
                    ins.then_inc(s["sh_done"], 1)

            def proj_bias(st, has_v):
                pe.wait_ge(s["vdup_ready"], has_v)
                if not isinstance(st, int) or st >= 1:
                    pe.wait_ge(s["sh_read"], st)
                t.matmul(bA[:], row0[:], b2s_mat[:].rearrange("p t d -> p (t d)"), start=True, stop=False,
                         skip_group_check=True)

            def out_part(st, part):
                pe.wait_ge(s["z_ready"], 4 * st + part + 1)
                for d in (2 * part, 2 * part + 1):
                    for j in range(TILES):
                        ins = t.matmul(bO[:, j * D:(j + 1) * D], Z[:, d, j * P:(j + 1) * P], wout_rot[:, d],
                                       start=False, stop=True, skip_group_check=True)
                if part == 3:
                    ins.then_inc(s["out_done"], 1)

            def iteration(i, head, tail, nxt, shared, first=False):
                again = not first
                sa = not isinstance(i, int) or i > 2
                if shared:
                    proj_bias(i - 2, (i + 1) if head else NS)
                    fc(i - 2, 0, sa)
                if head:
                    pe.wait_ge(s["vdup_ready"], i + 1)
                    v_rotated(i, 0, again)
                    v_rotated(i, 1, again)
                if shared:
                    fc(i - 2, 1, sa)
                    proj(i - 2, 0)
                if head:
                    v_rotated(i, 2, again)
                    pe.wait_ge(s["p_ready"], i + 1)
                    for j in range(TILES):
                        ins = t.matmul(ps_den[:, j * H:(j + 1) * H], pden[:, j * P:(j + 1) * P], head_ones[:],
                                       start=True, stop=True)
                    ins.then_inc(s["den_done"], 1)
                    v_rotated(i, 3, again)
                    v_rotated(i, 4, again)
                if shared:
                    fc(i - 2, 2, sa)
                    proj(i - 2, 1)
                if head:
                    v_rotated(i, 5, again)
                    pe.wait_ge(s["rden_ready"], i + 1)
                    pe.wait_ge(s["qk_read"], i + 1)
                    for j in range(TILES):
                        ins = t.transpose(bB[:, j * P:(j + 1) * P],
                                          rden8[:, j].rearrange("p e h -> p (e h)"), ident[:])
                    ins.then_inc(s["exp_done"], 1)
                if shared:
                    fc(i - 2, 3, sa)
                    proj(i - 2, 2)
                if head:
                    v_rotated(i, 6, again)
                    v_rotated(i, 7, again)
                if shared:
                    proj(i - 2, 3)
                if tail:
                    if head:
                        pe.wait_ge(s["xnt_ready"], i + 1)
                    ln_transposes(lambda j: rows[:, 0, j, 0:D], TILES, "xn2_ready", 4 * i, "t2_done")
                if head:
                    if again:
                        pe.wait_ge(s["attn_ready"], 4 * i)
                    t.matmul(bO[:], row0[:], bo_mat[:].rearrange("p t d -> p (t d)"), start=True, stop=False,
                             skip_group_check=True)
                    out_part(i, 0)
                if tail:
                    pe.wait_ge(s["xt2_ready"], i)
                    for j in range(TILES):
                        ins = t.matmul(ps_lg[:, j * NE:(j + 1) * NE], xt2[:, j * P:(j + 1) * P], wr_sb[:],
                                       start=True, stop=True)
                    ins.then_inc(s["lg_done"], 1)
                if head:
                    out_part(i, 1)
                if tail:
                    pe.wait_ge(s["chosen_ready"], i)
                    if not isinstance(i, int) or i > 1:
                        pe.wait_ge(s["acc_ready"], i - 1)
                    rk = ps_rank.rearrange("p (t e) -> p t e", t=TILES)
                    t.matmul(ps_rank, before[:], chosen[:].rearrange("p t e -> p (t e)"), start=True,
                             stop=False, skip_group_check=True)
                    for j in range(TILES - 1):
                        n = TILES - 1 - j
                        t.matmul(rk[:, j + 1:, :], ones_bf[:],
                                 chosen[:, j, :].unsqueeze(1).broadcast_to([P, n, NE]), start=False, stop=False,
                                 skip_group_check=True)
                    t.matmul(rk, ones_bf[:], chosen_acc[:].unsqueeze(1).broadcast_to([P, TILES, NE]), start=False,
                             stop=True, skip_group_check=True).then_inc(s["rank_done"], 1)
                if nxt:
                    project(i + 1, True)
                if head:
                    out_part(i, 2)
                    out_part(i, 3)

            pe.wait_ge(s["w_rest"], 48)
            pe.wait_ge(s["b2s_in"], 16 * TILES)
            iteration(0, True, False, True, False, first=True)
            iteration(1, True, True, True, False)
            iteration(2, True, True, True, True)
            with pe.Fori(3, NS - 1) as i:
                iteration(i, True, True, True, True)
            iteration(NS - 1, True, True, False, True)
            iteration(NS, False, True, False, True)
            st = NS - 1
            pe.wait_ge(s["acc_ready"], NS)
            pe.wait_ge(s["place_ready"], NS)
            t.matmul(bS[:, 0:NE], ones_bf[:], chosen_acc[:], start=True, stop=True).then_inc(s["cnt_done"], 1)
            proj_bias(st, NS)
            for c in range(CH):
                fc(st, c, True)
                proj(st, c)
            pe.wait_ge(s["tab"], 1)
            pe.wait_ge(s["sh_read"], NS)

            def rows_in(b, buf, par, again):
                pe.wait_ge(xb_in[buf], 16 * turn(b, buf) + 16)
                if again:
                    pe.wait_ge(s["blk_tr"], b - 1)
                for c in range(2):
                    ins = t.transpose(blk_t[par][:, c * P:(c + 1) * P], xb[buf][:, c, 0:D], ident[:])
                ins.then_inc(s["blk_tp"], 1)

            def turn(b, buf):
                return (b - buf) // NBUF if isinstance(b, int) else turns[0]

            turns = [None]

            def hidden(b, buf, par, again):
                pe.wait_ge(wb_in[buf], 16 * turn(b, buf) + 16)
                pe.wait_ge(s["blk_tr"], b + 1)
                if again:
                    pe.wait_ge(s["blk_gelu"], b - 1)
                for c in range(CH):
                    ins = t.matmul(blk_h[par][c // 2][:, (c % 2) * BLK:(c % 2 + 1) * BLK],
                                   wb[buf][:, c * P:(c + 1) * P], xbt[buf][:], start=True, stop=True)
                ins.then_inc(s["blk_fc"], 1)

            def second(b, buf, par, again):
                pe.wait_ge(s["blk_gelu"], b + 1)
                if again:
                    pe.wait_ge(s["blk_yr"], b - 1)
                for c in range(CH):
                    for r in range(2):
                        ins = t.matmul(blk_y[par][:, r * D:(r + 1) * D], hb[buf][:, c, r * P:(r + 1) * P],
                                       wb[buf][:, HID + c * D:HID + (c + 1) * D],
                                       start=(c == 0 and r == 0), stop=True, skip_group_check=True)
                ins.then_inc(s["blk_mm2"], 1)

            rows_in(0, 0, 0, False)
            hidden(0, 0, 0, False)
            span = 2 * NBUF
            loops = (NB - 1 - NBUF) // span

            def step(b, n, again):
                rows_in(b, n % NBUF, n % 2, again)
                hidden(b, n % NBUF, n % 2, again)
                second(b - 1, (n - 1) % NBUF, (n - 1) % 2, n >= 3)

            for n in range(1, NBUF):
                step(n, n, n >= 2)
            with pe.Fori(0, loops) as it:
                for n in range(span):
                    turns[0] = it * 2 + 1 + n // NBUF
                    b = it * span + NBUF + n
                    rows_in(b, n % NBUF, (NBUF + n) % 2, True)
                    hidden(b, n % NBUF, (NBUF + n) % 2, True)
                    second(b - 1, (n - 1) % NBUF, (NBUF + n - 1) % 2, True)
            for b in range(NBUF + loops * span, NB):
                step(b, b, True)
            second(NB - 1, (NB - 1) % NBUF, (NB - 1) % 2, True)

        @block.vector
        def _(dve):
            v = nc.vector
            dve.wait_ge(s["consts"], 4)
            dve.wait_ge(s["bias_in"], 64)
            v.tensor_copy(bqkv_rows[:], bqkv_raw[:].rearrange("r (h e) -> r e h", h=H)
                          ).then_inc(s["setup_dve"], 1)
            for j in range(TILES):
                v.tensor_copy(bv_mat[0:1, j, :].rearrange("p (e h) -> p e h", e=E),
                              bv_raw[:].rearrange("p (h e) -> p e h", h=H))
            v.tensor_reduce(head_ones[:], ident[:].rearrange("p (e h) -> p h e", e=E), AX_X, ALU.add)
            dve.wait_ge(s["w_first"], 32)
            for m in range(3):
                ins = v.tensor_copy(wqkv_sb[:, m], wqkv_raw[:, m * D:(m + 1) * D].rearrange("p (h e) -> p e h", h=H))
            ins.then_inc(s["setup_dve"], 1)
            dve.wait_ge(s["setup_pe"], 1)
            v.tensor_copy(bias_cols[:], bS[:, 0:NBIAS])
            v.tensor_copy(bk_col[:], bS[:, 65:66])
            v.tensor_scalar(bq_scaled[:], bS[:, 64:65], E ** -0.5, None, ALU.mult).then_inc(s["setup_dve"], 1)
            dve.wait_ge(s["setup_dve"], 3)
            v.tensor_copy(b12[:, :, 0:CH], bias_cols[:, 0:NE * CH].rearrange("p (e c) -> p e c", e=NE))
            dve.wait_ge(s["setup_pe"], 2)
            for half in range(2):
                ins = v.tensor_copy(wout_t[:, half], bO[:, 0:D].rearrange("p (h e) -> p e h", h=H))
            ins.then_inc(s["setup_dve"], 1)

            def stats(which, src, done, mid, value):
                for j in range(TILES):
                    ins = v.bn_stats(bst[:, which, j], src(j))
                ins.then_inc(s[mid], 1)
                dve.wait_ge(s[mid], value)
                alone(dve)
                for j in range(TILES):
                    ins = v.bn_aggr(mv[:, which, j], bst[:, which, j])
                ins.then_inc(s[done], 1)

            def normal(which, dst, src, rdy, value, done):
                dve.wait_ge(s[rdy], value)
                for j in range(TILES):
                    v.tensor_scalar(dst(j), src(j), mv[:, which, j, 0:1], rstd[:, which, j:j + 1],
                                    ALU.subtract, ALU.mult).then_inc(s[done], 1)

            def Xt(st, j):
                if isinstance(st, int):
                    return X[:, TILES * st + j, :]
                return X[:, bass.ds(TILES * st + j, 1), :].rearrange("p o d -> p (o d)")

            def ln0_stats(st):
                stats(0, lambda j: Xt(st, j), "ln0_mv", "ln0_st", st + 1)

            def ln0_apply(st, again):
                if again:
                    dve.wait_ge(s["t0_done"], st)
                normal(0, lambda j: xn[:, j], lambda j: Xt(st, j), "ln0_rstd", st + 1, "xn_ready")

            dve.wait_ge(s["x_first"], 16)
            ln0_stats(0)
            ln0_apply(0, False)
            dve.wait_ge(s["setup_pe"], 3)
            for half in range(2):
                ins = v.tensor_copy(wout_rot[:, 4 * half:4 * half + 4],
                                    bV[half][:].rearrange("p (a d) -> p a d", a=4))
            ins.then_inc(s["setup_dve"], 1)
            dve.wait_ge(s["x_rest"], 16)

            def prod(i, d):
                dve.wait_ge(s["vt_done"], E * i + d + 1)
                v.scalar_tensor_tensor(out=KV[:, d], in0=qk0[:, 1], scalar=FEAT_EPS, in1=bV[d % 2][:],
                                       op0=ALU.add, op1=ALU.mult).then_inc(s["kv_prod"], 1)

            def sums(i, part):
                dve.wait_ge(s["kv_prod"], E * i + 2 * part + 2)
                w = KV[:, 2 * part:2 * part + 2].rearrange("p a t -> p (a t)")
                v.tensor_tensor_scan(w, keep[:], w, 0.0, ALU.mult, ALU.add).then_inc(s["kv_sum"], 1)

            def zed(i, part):
                dve.wait_ge(s["kv_sum"], 4 * i + part + 1)
                v.tensor_tensor(Z[:, 2 * part:2 * part + 2], KV[:, 2 * part:2 * part + 2],
                                qn[:].unsqueeze(1).broadcast_to([P, 2, STEP]), ALU.mult).then_inc(s["z_ready"], 1)

            def iteration(i, head, tail, nxt, first=False):
                again = not first
                late = not isinstance(i, int) or i > 1
                if head:
                    dve.wait_ge(s["qk_read"], i + 1)
                    if again:
                        dve.wait_ge(s["k1_ready"], i)
                    v.scalar_tensor_tensor(out=qk0[:], in0=e_qk[:], scalar=1.0, in1=r_qk[:], op0=ALU.min,
                                           op1=ALU.add).then_inc(s["qk_ready"], 1)
                    dve.wait_ge(s["qk_ready"], i + 1)
                    prod(i, 0)
                    prod(i, 1)
                    dve.wait_ge(s["k1_ready"], i + 1)
                    v.tensor_tensor_scan(KC[:], keep[:, 0:STEP], k1[:], 0.0, ALU.mult,
                                         ALU.add).then_inc(s["kc_ready"], 1)
                if tail:
                    dve.wait_ge(s["out_done"], i)
                    stats(1, lambda j: bO[:, j * D:(j + 1) * D], "ln1_mv", "ln1_st", i)
                if head:
                    prod(i, 2)
                    dve.wait_ge(s["kc_ready"], i + 1)
                    if again:
                        dve.wait_ge(s["den_done"], i)
                    v.scalar_tensor_tensor(out=pden[:], in0=qk0[:, 0], scalar=FEAT_EPS, in1=KC[:], op0=ALU.add,
                                           op1=ALU.mult).then_inc(s["p_ready"], 1)
                    prod(i, 3)
                    sums(i, 0)
                if tail:
                    if late:
                        dve.wait_ge(s["x1_ready"], i - 1)
                    normal(1, lambda j: attn[:, j], lambda j: bO[:, j * D:(j + 1) * D], "ln1_rstd", i,
                           "attn_ready")
                if head:
                    dve.wait_ge(s["den_done"], i + 1)
                    v.tensor_scalar(den[:], ps_den, DEN_EPS, None, ALU.add).then_inc(s["den_add"], 1)
                    prod(i, 4)
                    dve.wait_ge(s["den_add"], i + 1)
                    v.reciprocal(rden[:].rearrange("p t h -> p (t h)"), den[:]).then_inc(s["den_inv"], 1)
                    prod(i, 5)
                    dve.wait_ge(s["den_inv"], i + 1)
                    if again:
                        dve.wait_ge(s["exp_done"], i)
                    for j in range(TILES):
                        ins = v.tensor_copy(rden8[:, j], rden[:, j].unsqueeze(1).broadcast_to([P, E, H]))
                    ins.then_inc(s["rden_ready"], 1)
                    sums(i, 1)
                if tail:
                    dve.wait_ge(s["x1_ready"], i)
                    stats(2, lambda j: Xt(i - 1, j), "ln2_mv", "ln2_st", i)
                if head:
                    dve.wait_ge(s["exp_done"], i + 1)
                    v.scalar_tensor_tensor(out=qn[:], in0=qk0[:, 0], scalar=FEAT_EPS, in1=bB[:], op0=ALU.add,
                                           op1=ALU.mult).then_inc(s["qn_ready"], 1)
                    prod(i, 6)
                    prod(i, 7)
                    sums(i, 2)
                    sums(i, 3)
                if tail:
                    if late:
                        dve.wait_ge(s["scattered"], 16 * 2 * TILES * (i - 1))
                    dst = dest[:, i - 1] if isinstance(i, int) else \
                        dest[:, bass.ds(i - 1, 1)].rearrange("p o k t -> p (o k) t")
                    v.tensor_copy(rows[:].bitcast(I32)[:, :, :, D:ROW].rearrange("p k t o -> p k (t o)"),
                                  dst).then_inc(s["dest_ready"], 1)
                    normal(2, lambda j: rows[:, 0, j, 0:D], lambda j: Xt(i - 1, j), "ln2_rstd", i, "xn2_ready")
                if head:
                    dve.wait_ge(s["qn_ready"], i + 1)
                    if again:
                        dve.wait_ge(s["out_done"], i)
                    zed(i, 0)
                if nxt:
                    ln0_stats(i + 1)
                if head:
                    zed(i, 1)
                if tail:
                    dve.wait_ge(s["lg_done"], i)
                    v.tensor_copy(lg[:], ps_lg.rearrange("p (t e) -> p t e", t=TILES)).then_inc(s["lg_read"], 1)
                if nxt:
                    ln0_apply(i + 1, True)
                if tail:
                    dve.wait_ge(s["lg_read"], i)
                    alone(dve)
                    for j in range(TILES):
                        v.max(top[:, j], lg[:, j]).then_inc(s["top_ready"], 1)
                    for j in range(TILES):
                        dve.wait_ge(s["top_ready"], 2 * TILES * (i - 1) + j + 1)
                        alone(dve)
                        v.max_index(topi[:, j], top[:, j], lg[:, j]).then_inc(s["top_ready"], 1)
                    g = gap[:, bass.ds(TILES * (i - 1), TILES)]
                    v.tensor_tensor(g, top[:, :, 1], top[:, :, 0], ALU.subtract)
                    dve.wait_ge(s["top_ready"], 2 * TILES * i)
                    v.tensor_copy(idxf[:], topi[:, :, 0:2].rearrange("p t k -> p k t")
                                  ).then_inc(s["idx_ready"], 1)
                    dve.wait_ge(s["idx_ready"], i)
                    v.tensor_tensor(onehot[:].rearrange("p k t e -> p (k t) e"),
                                    idxf[:].rearrange("p k t -> p (k t)").unsqueeze(2)
                                    .broadcast_to([P, 2 * TILES, NE]),
                                    iota8[:].unsqueeze(1).broadcast_to([P, 2 * TILES, NE]),
                                    ALU.is_equal).then_inc(s["hot_ready"], 1)
                    dve.wait_ge(s["hot_ready"], i)
                    if late:
                        dve.wait_ge(s["rank_done"], i - 1)
                    v.tensor_tensor(chosen[:], onehot[:, 0], onehot[:, 1], ALU.add).then_inc(s["chosen_ready"], 1)
                if head:
                    zed(i, 2)
                if tail:
                    dve.wait_ge(s["chosen_ready"], i)
                    v.tensor_reduce(chosen_sum[:], chosen[:].rearrange("p t e -> p e t"), AX_X,
                                    ALU.add).then_inc(s["acc_red"], 1)
                    dve.wait_ge(s["rank_done"], i)
                    v.tensor_tensor(place[:], ps_rank.rearrange("p (t e) -> p t e", t=TILES),
                                    list_base[:].unsqueeze(1).broadcast_to([P, TILES, NE]),
                                    ALU.add).then_inc(s["place_ready"], 1)
                    dve.wait_ge(s["acc_red"], i)
                    v.tensor_tensor(chosen_acc[:], chosen_acc[:], chosen_sum[:], ALU.add
                                    ).then_inc(s["acc_ready"], 1)
                    dve.wait_ge(s["place_ready"], i)
                    v.tensor_tensor(placed[:], onehot[:], place[:].unsqueeze(1).broadcast_to([P, 2, TILES, NE]),
                                    ALU.mult).then_inc(s["placed_ready"], 1)
                if head:
                    zed(i, 3)
                if tail:
                    dve.wait_ge(s["placed_ready"], i)
                    v.tensor_reduce(posf[:], placed[:].rearrange("p k t e -> p (k t) e"), AX_X,
                                    ALU.add).then_inc(s["posf_ready"], 1)
                    dve.wait_ge(s["posf_ready"], i)
                    if late:
                        dve.wait_ge(s["scattered"], 16 * 2 * TILES * (i - 1))
                    v.tensor_copy(pos[:], posf[:]).then_inc(s["pos_ready"], 1)

            iteration(0, True, False, True, first=True)
            iteration(1, True, True, True)
            with dve.Fori(2, NS - 1) as i:
                iteration(i, True, True, True)
            iteration(NS - 1, True, True, False)
            iteration(NS, False, True, False)

            n = [0]

            def link(ins):
                n[0] += 1
                ins.then_inc(s["tab"], 1)
                dve.wait_ge(s["tab"], n[0])

            M = LIST // BLK - 1
            dve.wait_ge(s["cnt_done"], 1)
            link(v.tensor_copy(cnt[:], bS[0:1, 0:NE]))
            link(v.tensor_tensor(full16[:], cnt[:].unsqueeze(2).broadcast_to([1, NE, M]), steps16[:], ALU.is_gt))
            link(v.tensor_reduce(nblk[:], full16[:], AX_X, ALU.add))
            link(v.tensor_tensor_scan(cum[:], one8[:], nblk[:], 0.0, ALU.mult, ALU.add))
            link(v.tensor_scalar(jump[:], nblk[:], -float(BLK), float(LIST), ALU.mult, ALU.add))
            link(v.tensor_tensor(past[:], bnum[:], cum[:].unsqueeze(1).broadcast_to([1, NB, NE]), ALU.is_ge))
            link(v.tensor_reduce(tabf[:, 0:NB], past[:], AX_X, ALU.add))
            link(v.tensor_scalar(tabf[:, 0:NB], tabf[:, 0:NB], float(NE - 1), None, ALU.min))
            link(v.tensor_tensor(pastj[:], past[:], jump[:].unsqueeze(1).broadcast_to([1, NB, NE]), ALU.mult))
            link(v.tensor_reduce(tabf[:, NB:2 * NB], pastj[:], AX_X, ALU.add))
            link(v.tensor_tensor(tabf[:, NB:2 * NB], tabf[:, NB:2 * NB], b256[:], ALU.add))
            link(v.tensor_tensor(tabf[:, 2 * NB:2 * NB + NE], cnt[:], list_base[0:1, :], ALU.add))
            v.tensor_copy(table[:], tabf[:, 0:2 * NB + NE]).then_inc(s["table_ready"], 1)

            def rows_read(b, buf, par, again):
                dve.wait_ge(s["blk_tp"], b + 1)
                if again:
                    dve.wait_ge(s["blk_fc"], b - NBUF + 1)
                v.tensor_copy(xbt[buf][:], blk_t[par]).then_inc(s["blk_tr"], 1)

            def result_read(b, buf, par, turn):
                dve.wait_ge(s["blk_mm2"], b + 1)
                if turn is not None:
                    dve.wait_ge(blk_scat[buf], 32 * turn)
                v.tensor_tensor(yb[buf][:], blk_y[par][:, 0:2 * D].rearrange("p (r d) -> p r d", r=2),
                                wb[buf][:, B2_AT:WROW].unsqueeze(1).broadcast_to([P, 2, D]),
                                ALU.add).then_inc(s["blk_yr"], 1)

            rows_read(0, 0, 0, False)
            for b in range(1, NBUF):
                rows_read(b, b, b % 2, False)
                result_read(b - 1, b - 1, (b - 1) % 2, None)
            b = NBUF
            rows_read(b, 0, b % 2, True)
            result_read(b - 1, NBUF - 1, (b - 1) % 2, None)
            span = 2 * NBUF
            loops = (NB - b - 1) // span
            with dve.Fori(0, loops) as it:
                for m in range(span):
                    c = it * span + (b + 1) + m
                    rows_read(c, (b + 1 + m) % NBUF, (b + 1 + m) % 2, True)
                    result_read(c - 1, (b + m) % NBUF, (b + m) % 2, it * 2 + (b + m) // NBUF)
            for c in range(b + 1 + loops * span, NB):
                rows_read(c, c % NBUF, c % 2, True)
                result_read(c - 1, (c - 1) % NBUF, (c - 1) % 2, (c - 1) // NBUF)
            result_read(NB - 1, (NB - 1) % NBUF, (NB - 1) % 2, (NB - 1) // NBUF)

            dve.wait_ge(s["gate_exp"], 1)
            v.tensor_scalar(gates[:, 0], gates[:, 1], 1.0, None, ALU.add).then_inc(s["gate_w"], 1)
            dve.wait_ge(s["gate_w"], 1)
            v.reciprocal(gates[:, 0], gates[:, 0]).then_inc(s["gate_w"], 1)
            dve.wait_ge(s["gate_w"], 2)
            v.tensor_tensor(gates[:, 1], gates[:, 1], gates[:, 0], ALU.mult).then_inc(s["gate_w"], 1)
            dve.wait_ge(s["gate_w"], 3)

            def combine(g):
                f, y, m = fin[:, g % NFIN], Y[:, g % NFIN], g % NFIN
                dve.wait_ge(y_in[g], 16)
                if g >= NFIN:
                    dve.wait_ge(out_stored[g - NFIN], 16)
                for k, done in enumerate(("fin_y0", "fin_y1")):
                    for j in range(TILES):
                        n = TILES * g + j
                        ins = v.scalar_tensor_tensor(out=f[:, j], in0=y[:, j, k], scalar=gates[:, k, n:n + 1],
                                                     in1=SH[:, n] if k == 0 else f[:, j], op0=ALU.mult,
                                                     op1=ALU.add)
                    ins.then_inc(s[done], 1)
                    dve.wait_ge(s[done], g + 1)
                for j in range(TILES):
                    ins = v.bn_stats(bst[:, m, j], f[:, j])
                ins.then_inc(s["fin_st"], 1)
                dve.wait_ge(s["fin_st"], g + 1)
                for j in range(TILES):
                    ins = v.bn_aggr(mv[:, m, j], bst[:, m, j])
                ins.then_inc(s["fin_mv"], 1)
                dve.wait_ge(s["fin_mv"], g + 1)
                v.tensor_scalar(ve[:, m], mv[:, m, :, 1], LN_EPS, None, ALU.add).then_inc(s["fin_ve"], 1)

            def finish(g):
                f, m = fin[:, g % NFIN], g % NFIN
                dve.wait_ge(s["fin_rstd"], g + 1)
                for j in range(TILES):
                    ins = v.tensor_scalar(f[:, j], f[:, j], mv[:, m, j, 0:1], rstd[:, m, j:j + 1], ALU.subtract,
                                          ALU.mult)
                ins.then_inc(s["fin_n"], 1)
                dve.wait_ge(s["fin_n"], g + 1)
                v.tensor_tensor(f, f, X[:, TILES * g:TILES * (g + 1)], ALU.add).then_inc(s["fin_done"], 1)

            combine(0)
            for g in range(1, NS):
                combine(g)
                finish(g - 1)
            finish(NS - 1)


_INS = ['L0_attn_x', 'L0_attn_W_qkv', 'L0_attn_b_qkv', 'L0_attn_W_out', 'L0_attn_b_out', 'L0_ffn_Wfc_s',
        'L0_ffn_bfc_s', 'L0_ffn_Wproj_s', 'L0_ffn_bproj_s', 'L0_ffn_Wr', 'L0_ffn_Wfc', 'L0_ffn_bfc',
        'L0_ffn_Wproj', 'L0_ffn_bproj']


def kernel(**inputs):
    import numpy as _np
    import concourse.bacc as _bacc
    from concourse import mybir as _mybir
    from concourse.bass_utils import run_bass_kernel_spmd as _run

    nc = _bacc.Bacc("TRN2", target_bir_lowering=False, num_devices=1)
    arrays, args = {}, []
    for name in _INS:
        a = _np.ascontiguousarray(inputs[name])
        arrays[f"in_{name}"] = a
        args.append(nc.dram_tensor(f"in_{name}", a.shape, _mybir.dt.from_np(a.dtype), kind="ExternalInput").ap())
    shape = inputs['L0_attn_x'].shape
    args.append(nc.dram_tensor("out_0", shape, _mybir.dt.float32, kind="ExternalOutput").ap())
    sandwich_kernel(nc, *args)
    r = _run(nc, [arrays], core_ids=[0])
    return r.results[0]["out_0"]
```

```python
from contextlib import ExitStack

import concourse.bass as bass
from concourse import mybir

ALU = mybir.AluOpType
ACT = mybir.ActivationFunctionType
F32 = mybir.dt.float32
BF16 = mybir.dt.bfloat16
F32R = mybir.dt.float32r
I32 = mybir.dt.int32
U32 = mybir.dt.uint32
AX_X = mybir.AxisListType.X

P = 128
D = 128
H, E = 16, 8
L = 256
TILES = 4
STEP = TILES * P
HID = 512
CH = HID // P
NE = 8
BLK = 256
FEAT_EPS = 1e-4
DEN_EPS = 1e-6
LN_EPS = 1e-5


def sandwich_kernel(nc, x, w_qkv, b_qkv, w_out, b_out, wfc_s, bfc_s, wproj_s, bproj_s, wr, wfc, bfc, wproj,
                    bproj, out):
    x_rows = x.rearrange("b l d -> (b l) d")
    out_rows = out.rearrange("b l d -> (b l) d")
    TOKENS = x_rows.shape[0]
    NS = TOKENS // STEP
    NT = TOKENS // P
    PAIRS = 2 * TOKENS
    NB = PAIRS // BLK + NE - 1
    SPARE = NB - PAIRS // BLK
    LIST = TOKENS + BLK
    ROW = D + 1
    WROW = HID + CH * D + CH + D
    B1_AT = HID + CH * D
    B2_AT = B1_AT + CH
    PADS = NE + SPARE
    NBUF = 6

    lists = nc.dram_tensor("expert_lists", [NE * LIST + SPARE * BLK, ROW], F32).ap()
    results = nc.dram_tensor("expert_results", [PAIRS + PADS * BLK, D], F32).ap()
    packed = nc.dram_tensor("packed_weights", [NE, P, WROW], F32).ap()

    with ExitStack() as ctx:
        def sb(name, shape, dt=F32):
            return ctx.enter_context(nc.sbuf_tensor(name, shape, dt))

        def bank(name, shape, dt=F32):
            return ctx.enter_context(nc.psum_tensor(name, shape, dt))

        def sem(name):
            return ctx.enter_context(nc.semaphore(name))

        ident = sb("ident", [P, P])
        ones3 = sb("ones3", [P, P], BF16)
        head_ones = sb("head_ones", [P, H])
        before = sb("before", [P, P], BF16)
        ones_bf = sb("ones_bf", [P, P], BF16)
        keep = sb("keep", [P, 2 * STEP], BF16)
        iota8 = sb("iota8", [P, NE])
        list_base = sb("list_base", [P, NE])
        dest = sb("dest", [P, NS, 2, TILES], I32)
        neg_half = sb("neg_half", [P, TILES])
        ln_eps = sb("ln_eps", [P, TILES])
        minus_one = sb("minus_one", [P, TILES])
        wqkv_raw = sb("wqkv_raw", [P, 3 * D])
        wqkv_sb = sb("wqkv_sb", [P, 3, E, H])
        wout_sb = sb("wout_sb", [P, D])
        wout_t = sb("wout_t", [P, 2, E, H])
        wout_rot = sb("wout_rot", [P, E, D])
        wr_sb = sb("wr_sb", [P, NE])
        w1s_sb = sb("w1s_sb", [P, HID])
        w2s_sb = sb("w2s_sb", [P, CH, D])
        NBIAS = NE * CH + CH
        bias_rows = sb("bias_rows", [NBIAS, P])
        bias_cols = sb("bias_cols", [P, NBIAS])
        bqkv_raw = sb("bqkv_raw", [3, D])
        bqkv_rows = sb("bqkv_rows", [3, E, H])
        bq_scaled = sb("bq_scaled", [P, 1])
        bk_col = sb("bk_col", [P, 1])
        bias_raw = sb("bias_raw", [P, 3, D])
        bias_f = sb("bias_f", [P, 3, D])
        bias_part = [sb(f"bias_part{n}", [P, 3, D], BF16) for n in range(3)]
        bias3 = sb("bias3", [P, 3, D], BF16)
        b12 = sb("b12", [P, NE, CH + D])
        pads = sb("pads", [P, PADS, 2, ROW])
        X = sb("X", [P, NT, D])
        SH = sb("SH", [P, NT, D])
        bst = sb("bst", [P, 3, TILES, 6])
        mv = sb("mv", [P, 3, TILES, 2])
        ve = sb("ve", [P, 3, TILES])
        rstd = sb("rstd", [P, 3, TILES])
        neg_mean = sb("neg_mean", [P, 3, TILES])
        shift = sb("shift", [P, 3, TILES])
        xn = sb("xn", [P, TILES, D])
        xn_t = sb("xn_t", [P, STEP])
        e_qk = sb("e_qk", [P, 2, STEP])
        r_qk = sb("r_qk", [P, 2, STEP])
        qk0 = sb("qk0", [P, 2, STEP])
        k1 = sb("k1", [P, STEP])
        vdup = sb("vdup", [P, TILES, 2 * D])
        KV = sb("KV", [P, E, STEP])
        KC = sb("KC", [P, STEP])
        pden = sb("pden", [P, STEP])
        den = sb("den", [P, TILES * H])
        rden = sb("rden", [P, TILES, H])
        rden8 = sb("rden8", [P, TILES, E, H])
        qn = sb("qn", [P, STEP])
        Z = sb("Z", [P, E, STEP])
        attn = sb("attn", [P, TILES, D])
        rows = sb("rows", [P, 2, TILES, ROW])
        xn2 = sb("xn2", [P, TILES, D])
        xt2 = sb("xt2", [P, STEP])
        hs = sb("hs", [P, CH, STEP])
        lg = sb("lg", [P, TILES, NE])
        top = sb("top", [P, TILES, 8])
        topi = sb("topi", [P, TILES, 8], U32)
        idxf = sb("idxf", [P, 2, TILES])
        onehot = sb("onehot", [P, 2, TILES, NE])
        chosen = sb("chosen", [P, TILES, NE], BF16)
        chosen_sum = sb("chosen_sum", [P, NE])
        chosen_acc = sb("chosen_acc", [P, NE], BF16)
        gap = sb("gap", [P, NT])
        place = sb("place", [P, TILES, NE])
        placed = sb("placed", [P, 2, TILES, NE])
        posf = sb("posf", [P, 2 * TILES])
        pos = sb("pos", [P, 2 * TILES], I32)
        gates = sb("gates", [P, 2, NT])
        cnt = sb("cnt", [1, NE])
        steps16 = sb("steps16", [1, NE, LIST // BLK - 1])
        full16 = sb("full16", [1, NE, LIST // BLK - 1])
        nblk = sb("nblk", [1, NE])
        cum = sb("cum", [1, NE])
        one8 = sb("one8", [1, NE])
        jump = sb("jump", [1, NE])
        bnum = sb("bnum", [1, NB, NE])
        past = sb("past", [1, NB, NE])
        pastj = sb("pastj", [1, NB, NE])
        b256 = sb("b256", [1, NB])
        tabf = sb("tabf", [1, 2 * NB + NE])
        table = sb("table", [1, 2 * NB], I32)
        ends = sb("ends", [1, NE], I32)
        kvz = [w[:].rearrange("p a t -> p (a t)") for w in (KV, Z)]
        wb = [kvz[n // 3][:, (n % 3) * WROW:(n % 3 + 1) * WROW] for n in range(NBUF)]
        xb = [sb(f"xb{n}", [P, 2, ROW]) for n in range(NBUF)]
        x_hi = [sb(f"x_hi{n}", [P, BLK], F32R) for n in range(2)]
        x_lo = [sb(f"x_lo{n}", [P, BLK], F32R) for n in range(2)]
        w_hi = [sb(f"w_hi{n}", [P, HID], F32R) for n in range(2)]
        w_lo = [sb(f"w_lo{n}", [P, HID], F32R) for n in range(2)]
        hb = [hs[:].rearrange("p c (n t) -> p n c t", n=2)[:, n] for n in range(2)]
        yb = [sb(f"yb{n}", [P, 2, D]) for n in range(NBUF)]
        Y = [w.rearrange("p (n t k d) -> p n t k d", t=TILES, k=2, d=D) for w in kvz]
        PER_Y = Y[0].shape[1]

        bT = bank("bT", [P, STEP])
        bA = bank("bA", [P, STEP])
        bB = bank("bB", [P, STEP])
        bV = [bank(f"bV{n}", [P, STEP]) for n in range(2)]
        bO = bank("bO", [P, STEP])
        bS = bank("bS", [P, STEP])
        bH = bank("bH", [P, STEP])
        ps_den, ps_lg, ps_rank = bB[:, 0:TILES * H], bS[:, 64:64 + TILES * NE], bS[:, 128:128 + TILES * NE]
        blk_t = [bT[:, 0:BLK], bH[:, 0:BLK]]
        blk_h = [[bA, bB], [bV[0], bV[1]]]
        blk_y = [bO, bS]

        names = """waited x_first x_rest w_first w_rest bias_in rows_in b2_in bias_parts packed_w packed_b
            consts setup_pe setup_dve
            ln0_mv ln0_rstd xn_ready t0_done xnt_ready q_mm k_mm v_mm q_read qk_read vdup_ready qk_ready k1_ready
            vt_done kv_prod kc_ready kv_sum p_ready den_done den_add den_inv rden_ready exp_done qn_ready z_ready out_done
            ln1_st ln1_mv ve0_ready ve1_ready ve2_ready pow0_done pow1_done pow2_done ln1_rstd attn_ready x1_ready ln2_st ln2_mv ln2_rstd ln0_st
            xn2_ready dest_ready rows_ready t2_done xt2_ready
            fc_done gelu_done sh_done sh_read
            lg_done lg_read top_ready idx_ready hot_ready hot_both chosen_ready rank_done acc_red acc_ready
            place_ready placed_ready posf_ready pos_ready scattered
            pads_ready spare_in cnt_done tab table_ready ends_ready tails_in
            blk_tp blk_xhi blk_whi blk_wlo blk_tr blk_fc blk_gelu blk_mm2 blk_yr
            gate_exp gate_w fin_y0 fin_y1 fin_st fin_mv fin_ve fin_pow fin_shift fin_n fin_done out_stored""".split()
        s = {n: sem(n) for n in names}
        wb_in = [sem(f"wb_in{n}") for n in range(NBUF)]
        xb_in = [sem(f"xb_in{n}") for n in range(NBUF)]
        blk_scat = [sem(f"blk_scat{n}") for n in range(NBUF)]
        y_in = [sem(f"y_in{n}") for n in range(NS)]
        block = ctx.enter_context(nc.Block())

        def alone(eng):
            eng.sem_inc(s["waited"], 1)

        def over_blocks(eng, step, extra=0):
            def one(b, n, t):
                step(b, n, lambda k: t - (k > n))

            for b in range(NBUF):
                one(b, b, 0)
            with eng.Fori(1, NB // NBUF) as t:
                for n in range(NBUF):
                    one(t * NBUF + n, n, t)
            for b in range(NB - NB % NBUF, NB + extra):
                one(b, b % NBUF, b // NBUF)

        def Xt(st, j):
            if isinstance(st, int):
                return X[:, TILES * st + j, :]
            return X[:, bass.ds(TILES * st + j, 1), :].rearrange("p o d -> p (o d)")

        def all_iterations(eng, iteration):
            iteration(0, True, False, True, False)
            iteration(1, True, True, True, False)
            iteration(2, True, True, True, True)
            with eng.Fori(3, NS - 1) as i:
                iteration(i, True, True, True, True)
            iteration(NS - 1, True, True, False, True)
            iteration(NS, False, True, False, True)
            iteration(NS + 1, False, False, False, True)

        def from_on(b, first):
            return not isinstance(b, int) or b >= first

        def store(sp, g):
            sp.wait_ge(s["fin_done"], g + 1)
            sp.dma_start(out_rows[g * STEP:(g + 1) * STEP, :].rearrange("(t p) d -> p t d", p=P),
                         SH[:, TILES * g:TILES * (g + 1)]).then_inc(s["out_stored"], 16)

        @block.sync
        def _(sp):
            def xt(a, b):
                return x_rows[a * P:b * P, :].rearrange("(t p) d -> p t d", p=P)

            sp.dma_start(X[:, 0:TILES, :], xt(0, TILES)).then_inc(s["x_first"], 16)
            n = NE * CH
            sp.dma_start(bias_rows[0:n, :], bfc.rearrange("e (c p) -> (e c) p", p=P)).then_inc(s["bias_in"], 16)
            sp.dma_start(bias_rows[n:n + CH, :], bfc_s.rearrange("(c p) -> c p", p=P)).then_inc(s["bias_in"], 16)
            sp.dma_start(X[:, TILES:2 * TILES, :], xt(TILES, 2 * TILES)).then_inc(s["x_rest"], 16)
            sp.dma_start(w1s_sb[:], wfc_s).then_inc(s["w_rest"], 16)
            sp.dma_start(w2s_sb[:], wproj_s.rearrange("(c p) n -> p c n", p=P)).then_inc(s["w_rest"], 16)
            sp.dma_start(X[:, 2 * TILES:NT, :], xt(2 * TILES, NT)).then_inc(s["x_rest"], 16)
            sp.dma_start(b12[:, :, CH:CH + D], bproj.rearrange("(o e) d -> o e d", o=1).broadcast_to([P, NE, D])
                         ).then_inc(s["b2_in"], 16)
            for e in range(NE):
                sp.dma_start(packed[e, :, 0:HID], wfc[e]).then_inc(s["packed_w"], 16)
                sp.dma_start(packed[e, :, HID:B1_AT].rearrange("p (c n) -> p c n", c=CH),
                             wproj[e].rearrange("(c p) n -> p c n", p=P)).then_inc(s["packed_w"], 16)
            sp.wait_ge(s["b2_in"], 16)
            sp.wait_ge(s["setup_dve"], 4)
            sp.dma_start(packed[:, :, B1_AT:WROW].rearrange("e p n -> p e n"), b12[:]).then_inc(s["packed_b"], 16)
            sp.wait_ge(s["pads_ready"], 2)
            sp.dma_start(lists[NE * LIST:, :].rearrange("(c p) n -> p c n", p=P),
                         pads[:, NE:PADS, :, :].rearrange("p a c n -> p (a c) n")).then_inc(s["spare_in"], 16)
            sp.wait_ge(s["spare_in"], 16)
            sp.wait_ge(s["ends_ready"], 1)
            for e in range(NE):
                at = sp.value_load(ends[0:1, e:e + 1], min_val=e * LIST, max_val=e * LIST + TOKENS)
                sp.dma_start(lists[bass.ds(at, BLK), :].rearrange("(c p) n -> p c n", p=P),
                             pads[:, e, :, :]).then_inc(s["tails_in"], 16)
            sp.wait_ge(s["table_ready"], 1)
            sp.wait_ge(s["packed_w"], 16 * 2 * NE)
            sp.wait_ge(s["packed_b"], 16)

            def load_block(b, n, turn):
                who = sp.value_load(table[0:1, bass.ds(b, 1)], min_val=0, max_val=NE - 1)
                at = sp.value_load(table[0:1, bass.ds(b + NB, 1)], min_val=0,
                                   max_val=NE * LIST + (SPARE - 1) * BLK)
                if from_on(b, NBUF):
                    sp.wait_ge(s["blk_yr"], b - NBUF + 1)
                    alone(sp)
                sp.dma_start(wb[n], packed[bass.ds(who, 1), :, :].rearrange("e p n -> p (e n)")
                             ).then_inc(wb_in[n], 16)
                if isinstance(b, int) and b == 0:
                    sp.wait_ge(s["tails_in"], 16 * NE)
                    sp.wait_ge(s["scattered"], 16 * 2 * NT)
                if from_on(b, NBUF):
                    sp.wait_ge(blk_scat[n], 32 * turn(0))
                    alone(sp)
                sp.dma_start(xb[n][:], lists[bass.ds(at, BLK), :].rearrange("(c p) n -> p c n", p=P)
                             ).then_inc(xb_in[n], 16)

            over_blocks(sp, load_block)
            for n in range(NBUF):
                sp.wait_ge(blk_scat[n], 32 * ((NB - n + NBUF - 1) // NBUF))
            for g in range(NS):
                sp.dma_start(Y[g // PER_Y][:, g % PER_Y].rearrange("p t k d -> p t (k d)"),
                             results[2 * g * STEP:2 * (g + 1) * STEP, :]
                             .rearrange("(t p k) d -> p t (k d)", p=P, k=2)).then_inc(y_in[g], 16)
            for g in range(NS):
                store(sp, g)
            sp.wait_ge(s["out_stored"], 16 * NS)

        @block.gpsimd
        def _(pool):
            g = nc.gpsimd
            g.memset(bias_raw[:], 0.0).then_inc(s["consts"], 1)
            g.memset(bias3[:], 0.0)
            g.memset(ones3[:], 0.0)
            g.memset(ident[:], 0.0)
            g.memset(before[:], 1.0)
            g.memset(ones_bf[:], 1.0)
            g.memset(keep[:], 1.0)
            g.memset(neg_half[:], -0.5)
            g.memset(ln_eps[:], LN_EPS)
            g.memset(minus_one[:], -1.0)
            g.memset(chosen_acc[:], 0.0)
            g.memset(one8[:], 1.0).then_inc(s["consts"], 1)
            pool.wait_ge(s["consts"], 2)
            g.affine_select(out=ident[:], in_=ident[:], compare_op=ALU.not_equal, fill=1.0, base=0,
                            pattern=[[-1, P]], channel_multiplier=1)
            g.affine_select(out=before[:], in_=before[:], compare_op=ALU.is_gt, fill=0.0, base=0,
                            pattern=[[1, P]], channel_multiplier=-1).then_inc(s["consts"], 1)
            g.memset(keep[:].rearrange("p (a b) -> p a b", b=L)[:, :, 0:1], 0.0)
            g.iota(iota8[:], [[1, NE]], base=0, channel_multiplier=0, allow_small_or_imprecise_dtypes=True)
            g.iota(list_base[:], [[LIST, NE]], base=0, channel_multiplier=0,
                   allow_small_or_imprecise_dtypes=True)
            g.iota(dest[:], [[2 * STEP, NS], [1, 2], [2 * P, TILES]], base=0, channel_multiplier=2)
            g.iota(steps16[:], [[0, NE], [BLK, LIST // BLK - 1]], base=0, channel_multiplier=0,
                   allow_small_or_imprecise_dtypes=True)
            g.iota(bnum[:], [[1, NB], [0, NE]], base=0, channel_multiplier=0, allow_small_or_imprecise_dtypes=True)
            g.iota(b256[:], [[BLK, NB]], base=0, channel_multiplier=0,
                   allow_small_or_imprecise_dtypes=True).then_inc(s["consts"], 1)

            def inv_std(which, count):
                pool.wait_ge(s[f"ln{which}_mv"], count)
                g.tensor_tensor(ve[:, which], mv[:, which, :, 1], ln_eps[:], ALU.add)
                g.tensor_tensor(neg_mean[:, which], mv[:, which, :, 0], minus_one[:], ALU.mult
                                ).then_inc(s[f"ve{which}_ready"], 1)
                pool.wait_ge(s[f"ve{which}_ready"], count)
                g.tensor_tensor(rstd[:, which], ve[:, which], neg_half[:], ALU.pow
                                ).then_inc(s[f"pow{which}_done"], 1)
                pool.wait_ge(s[f"pow{which}_done"], count)
                g.tensor_tensor(shift[:, which], neg_mean[:, which], rstd[:, which], ALU.mult
                                ).then_inc(s[f"ln{which}_rstd"], 1)

            pool.wait_ge(s["consts"], 4)
            inv_std(0, 1)
            g.memset(pads[:], 0.0).then_inc(s["pads_ready"], 1)
            pool.wait_ge(s["pads_ready"], 1)
            g.iota(pads[:].bitcast(I32)[:, :, :, D:ROW], [[BLK, PADS], [P, 2], [0, 1]], base=PAIRS,
                   channel_multiplier=1).then_inc(s["pads_ready"], 1)

            def scatters(i, first, last):
                if first == 0:
                    pool.wait_ge(s["pos_ready"], i - 1)
                    pool.wait_ge(s["dest_ready"], i - 1)
                    pool.wait_ge(s["rows_ready"], i - 1)
                    alone(pool)
                for m in range(first, last):
                    g.indirect_dma_start(
                        out=lists, out_offset=bass.IndirectOffsetOnAxis(ap=pos[:, m:m + 1], axis=0),
                        in_=rows[:, m // TILES, m % TILES, :], in_offset=None).then_inc(s["scattered"], 16)

            def iteration(i, head, tail, nxt, routed):
                cuts = [0, 2, 4, 5, 2 * TILES] if tail and routed and not head else None
                if cuts:
                    scatters(i, cuts[0], cuts[1])
                if nxt:
                    inv_std(0, i + 2)
                if tail:
                    inv_std(1, i)
                    if cuts:
                        scatters(i, cuts[1], cuts[2])
                    pool.wait_ge(s["attn_ready"], i)
                    Xs = X[:, bass.ds(TILES * (i - 1), TILES), :]
                    g.tensor_tensor(Xs, Xs, attn[:], ALU.add).then_inc(s["x1_ready"], 1)
                    if cuts:
                        scatters(i, cuts[2], cuts[3])
                    inv_std(2, i)
                if cuts:
                    scatters(i, cuts[3], cuts[4])
                elif routed:
                    scatters(i, 0, 2 * TILES)

            all_iterations(pool, iteration)

            def scatter_block(b, n, turn):
                pool.wait_ge(s["blk_yr"], b + 1)
                alone(pool)
                for c in range(2):
                    g.indirect_dma_start(
                        out=results,
                        out_offset=bass.IndirectOffsetOnAxis(ap=xb[n][:].bitcast(I32)[:, c, D:ROW], axis=0),
                        in_=yb[n][:, c, :], in_offset=None).then_inc(blk_scat[n], 16)

            over_blocks(pool, scatter_block)
            def residual(n):
                pool.wait_ge(s["fin_n"], n + 1)
                f = SH[:, TILES * n:TILES * (n + 1)]
                g.tensor_tensor(f, f, X[:, TILES * n:TILES * (n + 1)], ALU.add).then_inc(s["fin_done"], 1)

            for n in range(NS):
                m = n % 3
                pool.wait_ge(s["fin_mv"], n + 1)
                g.tensor_tensor(ve[:, m], mv[:, m, :, 1], ln_eps[:], ALU.add)
                g.tensor_tensor(neg_mean[:, m], mv[:, m, :, 0], minus_one[:], ALU.mult).then_inc(s["fin_ve"], 1)
                if n >= 3:
                    pool.wait_ge(s["fin_n"], n - 2)
                pool.wait_ge(s["fin_ve"], n + 1)
                g.tensor_tensor(rstd[:, m], ve[:, m], neg_half[:], ALU.pow).then_inc(s["fin_pow"], 1)
                pool.wait_ge(s["fin_pow"], n + 1)
                g.tensor_tensor(shift[:, m], neg_mean[:, m], rstd[:, m], ALU.mult).then_inc(s["fin_shift"], 1)
                if n:
                    residual(n - 1)
            residual(NS - 1)

        @block.scalar
        def _(act):
            a = nc.scalar

            act.dma_start(wqkv_raw[:], w_qkv).then_inc(s["w_first"], 16)
            act.dma_start(bqkv_raw[:], b_qkv.rearrange("(c p) -> c p", p=P)).then_inc(s["bias_in"], 16)
            act.dma_start(wout_sb[:], w_out).then_inc(s["w_first"], 16)
            act.wait_ge(s["consts"], 1)
            for k, src in enumerate((b_qkv[2 * D:3 * D], b_out, bproj_s)):
                act.dma_start(bias_raw[0:96:32, k],
                              src.rearrange("(o d) -> o d", o=1).broadcast_to([3, D])).then_inc(s["rows_in"], 16)
            act.dma_start(wr_sb[:], wr).then_inc(s["w_rest"], 16)

            def normal(which, dst, src, ready, count):
                act.wait_ge(s[f"ln{which}_rstd"], count)
                for j in range(TILES):
                    ins = a.activation(dst(j), src(j), ACT.Identity, bias=shift[:, which, j:j + 1],
                                       scale=rstd[:, which, j:j + 1])
                ins.then_inc(s[ready], 1)

            def ln0_apply(st, again):
                if again:
                    act.wait_ge(s["t0_done"], st)
                normal(0, lambda j: xn[:, j], lambda j: Xt(st, j), "xn_ready", st + 1)

            def rows_to_project(st, again):
                act.wait_ge(s["t0_done"], st + 1)
                if again:
                    act.wait_ge(s["v_mm"], st)
                a.activation(xn_t[:], bT[:], ACT.Copy).then_inc(s["xnt_ready"], 1)

            def qk_maps(st, again):
                act.wait_ge(s["q_mm"], st + 1)
                if again:
                    act.wait_ge(s["qk_ready"], st)
                a.activation(e_qk[:, 0], bA[:], ACT.Exp, bias=bq_scaled[:], scale=E ** -0.5)
                a.activation(r_qk[:, 0], bA[:], ACT.Relu, bias=bq_scaled[:],
                             scale=E ** -0.5).then_inc(s["q_read"], 1)
                act.wait_ge(s["k_mm"], st + 1)
                a.activation(e_qk[:, 1], bB[:], ACT.Exp, bias=bk_col[:])
                a.activation(r_qk[:, 1], bB[:], ACT.Relu, bias=bk_col[:]).then_inc(s["qk_read"], 1)

            def v_twice(st, again):
                act.wait_ge(s["v_mm"], st + 1)
                if again:
                    act.wait_ge(s["vt_done"], E * st)
                v = bA[:].rearrange("p (t d) -> p t d", t=TILES)
                a.activation(vdup[:, :, 0:D], v, ACT.Copy)
                a.activation(vdup[:, :, D:2 * D], v, ACT.Copy).then_inc(s["vdup_ready"], 1)

            ln0_apply(0, False)
            rows_to_project(0, False)
            act.wait_ge(s["setup_dve"], 3)
            qk_maps(0, False)
            v_twice(0, False)

            def gelus(st, first, last):
                for c in range(first, last):
                    act.wait_ge(s["fc_done"], CH * st + c + 1)
                    a.activation(hs[:, c], bH[:], ACT.Gelu_apprx_tanh,
                                 bias=bias_cols[:, NE * CH + c:NE * CH + c + 1]).then_inc(s["gelu_done"], 1)

            def shared_out(st):
                act.wait_ge(s["sh_done"], st + 1)
                a.activation(SH[:, bass.ds(TILES * st, TILES), :], bA[:].rearrange("p (t d) -> p t d", t=TILES),
                             ACT.Copy).then_inc(s["sh_read"], 1)

            def iteration(i, head, tail, nxt, routed):
                if head:
                    act.wait_ge(s["qk_ready"], i + 1)
                    if from_on(i, 1):
                        act.wait_ge(s["kc_ready"], i)
                    a.activation(k1[:], qk0[:, 1], ACT.Copy, bias=FEAT_EPS).then_inc(s["k1_ready"], 1)
                if routed:
                    if head:
                        gelus(i - 2, 0, 1)
                    act.wait_ge(s["xn2_ready"], i - 1)
                    if from_on(i, 3):
                        act.wait_ge(s["scattered"], 16 * 2 * TILES * (i - 2))
                    for k in range(2):
                        ins = a.activation(rows[:, k, :, 0:D], xn2[:], ACT.Copy)
                    ins.then_inc(s["rows_ready"], 1)
                    gelus(i - 2, 1 if head else 0, 2)
                if nxt:
                    ln0_apply(i + 1, True)
                if routed and head:
                    gelus(i - 2, 2, 3)
                if nxt:
                    rows_to_project(i + 1, True)
                if tail:
                    if from_on(i, 2):
                        act.wait_ge(s["x1_ready"], i - 1)
                    normal(1, lambda j: attn[:, j], lambda j: bO[:, j * D:(j + 1) * D], "attn_ready", i)
                if routed:
                    gelus(i - 2, 3 if head else 2, 4)
                    shared_out(i - 2)
                if nxt:
                    qk_maps(i + 1, True)
                if tail:
                    if from_on(i, 2):
                        act.wait_ge(s["t2_done"], i - 1)
                    normal(2, lambda j: xn2[:, j], lambda j: Xt(i - 1, j), "xn2_ready", i)
                if nxt:
                    v_twice(i + 1, True)
                if tail:
                    act.wait_ge(s["t2_done"], i)
                    if from_on(i, 2):
                        act.wait_ge(s["fc_done"], CH * (i - 1))
                    a.activation(xt2[:], bT[:], ACT.Copy).then_inc(s["xt2_ready"], 1)

            all_iterations(act, iteration)

            def step(b, n, turn):
                if not isinstance(b, int) or b < NB:
                    act.wait_ge(wb_in[n], 16 * turn(0) + 16)
                    if from_on(b, 2):
                        act.wait_ge(s["blk_fc"], b - 1)
                    a.activation(w_hi[n % 2][:], wb[n][:, 0:HID], ACT.Copy).then_inc(s["blk_whi"], 1)
                if from_on(b, 1):
                    m = (n - 1) % NBUF
                    act.wait_ge(s["blk_fc"], b)
                    if from_on(b, 3):
                        act.wait_ge(s["blk_mm2"], b - 2)
                    for c in range(CH):
                        ins = a.activation(hb[m % 2][:, c],
                                           blk_h[m % 2][c // 2][:, (c % 2) * BLK:(c % 2 + 1) * BLK],
                                           ACT.Gelu_apprx_tanh, bias=wb[m][:, B1_AT + c:B1_AT + c + 1])
                    ins.then_inc(s["blk_gelu"], 1)

            over_blocks(act, step, extra=1)

            act.wait_ge(s["top_ready"], 2 * TILES * NS)
            act.wait_ge(s["idx_ready"], NS)
            a.activation(gates[:, 1], gap[:], ACT.Exp).then_inc(s["gate_exp"], 1)
            for n in range(NS):
                m = n % 3
                act.wait_ge(s["fin_shift"], n + 1)
                for j in range(TILES):
                    f = SH[:, TILES * n + j]
                    ins = a.activation(f, f, ACT.Identity, bias=shift[:, m, j:j + 1], scale=rstd[:, m, j:j + 1])
                ins.then_inc(s["fin_n"], 1)

        @block.tensor
        def _(pe):
            t = nc.tensor
            pe.wait_ge(s["consts"], 4)
            pe.wait_ge(s["bias_in"], 48)
            pe.wait_ge(s["setup_dve"], 1)
            t.transpose(bS[:, 0:NBIAS], bias_rows[:], ident[0:NBIAS, 0:NBIAS])
            t.transpose(bS[:, 64:67], bqkv_rows[:].rearrange("r e h -> r (e h)"), ident[0:3, 0:3]
                        ).then_inc(s["setup_pe"], 1)
            pe.wait_ge(s["w_first"], 32)
            t.transpose(bO[:, 0:D], wout_sb[:], ident[:]).then_inc(s["setup_pe"], 1)

            def transposes(src, done):
                for j in range(TILES):
                    ins = t.transpose(bT[:, j * P:(j + 1) * P], src[:, j], ident[:])
                ins.then_inc(s[done], 1)

            def add_bias(bank, which):
                t.matmul(bank[:].rearrange("p (t d) -> p t d", t=TILES), ones3[:],
                         bias3[:, which].unsqueeze(1).broadcast_to([P, TILES, D]), start=True, stop=False,
                         skip_group_check=True)

            def ln0_transposes(st):
                pe.wait_ge(s["xn_ready"], st + 1)
                if from_on(st, 3):
                    pe.wait_ge(s["xt2_ready"], st - 2)
                transposes(xn, "t0_done")

            def project(st, again):
                pe.wait_ge(s["xnt_ready"], st + 1)
                if from_on(st, 3):
                    pe.wait_ge(s["sh_read"], st - 2)
                t.matmul(bA[:], w3[:, 0:D], xn_t[:], start=True, stop=True).then_inc(s["q_mm"], 1)
                if again:
                    pe.wait_ge(s["qn_ready"], st)
                t.matmul(bB[:], w3[:, D:2 * D], xn_t[:], start=True, stop=True).then_inc(s["k_mm"], 1)
                pe.wait_ge(s["q_read"], st + 1)
                add_bias(bA, 0)
                for j in range(TILES):
                    ins = t.matmul(bA[:, j * D:(j + 1) * D], xn_t[:, j * P:(j + 1) * P], w3[:, 2 * D:3 * D],
                                   start=False, stop=True, skip_group_check=True)
                ins.then_inc(s["v_mm"], 1)

            pe.wait_ge(s["setup_dve"], 2)
            w3 = wqkv_sb[:].rearrange("p m e h -> p (m e h)")
            ln0_transposes(0)
            pe.wait_ge(s["bias_parts"], 7)
            project(0, False)
            pe.wait_ge(s["setup_dve"], 4)
            w2t = wout_t[:].rearrange("p a e h -> p (a e h)")
            for d in range(E):
                dst = bV[d // 4][:, (d % 4) * D:(d % 4 + 1) * D]
                ins = t.transpose(dst, w2t[:, d * H:d * H + D], ident[:])
            ins.then_inc(s["setup_pe"], 1)
            pe.wait_ge(s["setup_dve"], 5)

            def v_rotated(st, d, again):
                if again or d >= 2:
                    pe.wait_ge(s["kv_prod"], E * st + d - 1)
                for j in range(TILES):
                    ins = t.transpose(bV[d % 2][:, j * P:(j + 1) * P], vdup[:, j, d * H:d * H + D], ident[:])
                ins.then_inc(s["vt_done"], 1)

            def first_v(st, again):
                pe.wait_ge(s["vdup_ready"], st + 1)
                v_rotated(st, 0, again)
                v_rotated(st, 1, again)

            def fc(st, c, again):
                if again or c >= 1:
                    pe.wait_ge(s["gelu_done"], CH * st + c)
                t.matmul(bH[:], w1s_sb[:, c * P:(c + 1) * P], xt2[:], start=True,
                         stop=True).then_inc(s["fc_done"], 1)

            def proj(st, c):
                pe.wait_ge(s["gelu_done"], CH * st + c + 1)
                for j in range(TILES):
                    ins = t.matmul(bA[:, j * D:(j + 1) * D], hs[:, c, j * P:(j + 1) * P], w2s_sb[:, c],
                                   start=False, stop=True, skip_group_check=True)
                if c == CH - 1:
                    ins.then_inc(s["sh_done"], 1)

            def proj_bias(st):
                if from_on(st, 1):
                    pe.wait_ge(s["sh_read"], st)
                add_bias(bA, 2)

            def out_part(st, part):
                pe.wait_ge(s["z_ready"], 4 * st + part + 1)
                for d in (2 * part, 2 * part + 1):
                    for j in range(TILES):
                        ins = t.matmul(bO[:, j * D:(j + 1) * D], Z[:, d, j * P:(j + 1) * P], wout_rot[:, d],
                                       start=False, stop=True, skip_group_check=True)
                if part == 3:
                    ins.then_inc(s["out_done"], 1)

            def logits(i):
                if from_on(i, 3):
                    pe.wait_ge(s["acc_ready"], i - 2)
                for j in range(TILES):
                    ins = t.matmul(ps_lg[:, j * NE:(j + 1) * NE], xt2[:, j * P:(j + 1) * P], wr_sb[:],
                                   start=True, stop=True)
                ins.then_inc(s["lg_done"], 1)

            def ranks(i):
                pe.wait_ge(s["chosen_ready"], i - 1)
                rk = ps_rank.rearrange("p (t e) -> p t e", t=TILES)
                t.matmul(ps_rank, before[:], chosen[:].rearrange("p t e -> p (t e)"), start=True,
                         stop=False, skip_group_check=True)
                for j in range(TILES - 1):
                    n = TILES - 1 - j
                    t.matmul(rk[:, j + 1:, :], ones_bf[:],
                             chosen[:, j, :].unsqueeze(1).broadcast_to([P, n, NE]), start=False, stop=False,
                             skip_group_check=True)
                t.matmul(rk, ones_bf[:], chosen_acc[:].unsqueeze(1).broadcast_to([P, TILES, NE]), start=False,
                         stop=True, skip_group_check=True).then_inc(s["rank_done"], 1)

            def iteration(i, head, tail, nxt, routed):
                again = from_on(i, 1)
                ga = from_on(i, 3)
                if head:
                    v_rotated(i, 2, again)
                if routed:
                    pe.wait_ge(s["xt2_ready"], i - 1)
                    if not head and not tail:
                        logits(i)
                        ranks(i)
                        pe.wait_ge(s["acc_ready"], NS)
                        t.matmul(bS[:, 0:NE], ones_bf[:], chosen_acc[:], start=True, stop=True
                                 ).then_inc(s["cnt_done"], 1)
                    proj_bias(i - 2)
                    fc(i - 2, 0, ga)
                if head:
                    v_rotated(i, 3, again)
                if routed:
                    if head:
                        logits(i)
                    fc(i - 2, 1, ga)
                    proj(i - 2, 0)
                if head:
                    pe.wait_ge(s["qk_read"], i + 1)
                    pe.wait_ge(s["p_ready"], i + 1)
                    for j in range(TILES):
                        ins = t.matmul(ps_den[:, j * H:(j + 1) * H], pden[:, j * P:(j + 1) * P], head_ones[:],
                                       start=True, stop=True)
                    ins.then_inc(s["den_done"], 1)
                    v_rotated(i, 4, again)
                if routed:
                    fc(i - 2, 2, ga)
                    proj(i - 2, 1)
                if nxt:
                    ln0_transposes(i + 1)
                if head:
                    v_rotated(i, 5, again)
                if routed:
                    fc(i - 2, 3, ga)
                    proj(i - 2, 2)
                    if head:
                        ranks(i)
                    proj(i - 2, 3)
                if head:
                    pe.wait_ge(s["rden_ready"], i + 1)
                    for j in range(TILES):
                        ins = t.transpose(bB[:, j * P:(j + 1) * P],
                                          rden8[:, j].rearrange("p e h -> p (e h)"), ident[:])
                    ins.then_inc(s["exp_done"], 1)
                    v_rotated(i, 6, again)
                    v_rotated(i, 7, again)
                if nxt:
                    project(i + 1, True)
                if head:
                    if again:
                        pe.wait_ge(s["attn_ready"], i)
                    add_bias(bO, 1)
                    out_part(i, 0)
                if tail:
                    if nxt:
                        pe.wait_ge(s["xnt_ready"], i + 2)
                    pe.wait_ge(s["xn2_ready"], i)
                    transposes(xn2, "t2_done")
                if head:
                    out_part(i, 1)
                if nxt:
                    first_v(i + 1, True)
                if head and not nxt:
                    pe.wait_ge(s["xt2_ready"], i)
                    logits(i + 1)
                if head:
                    out_part(i, 2)
                if head and not nxt:
                    ranks(i + 1)
                if head:
                    out_part(i, 3)

            pe.wait_ge(s["w_rest"], 48)
            first_v(0, False)
            all_iterations(pe, iteration)
            pe.wait_ge(s["tab"], 1)
            pe.wait_ge(s["sh_read"], NS)

            def step(b, n, turn):
                if not isinstance(b, int) or b < NB:
                    pe.wait_ge(xb_in[n], 16 * turn(0) + 16)
                    if from_on(b, 2):
                        pe.wait_ge(s["blk_tr"], b - 1)
                    for c in range(2):
                        ins = t.transpose(blk_t[n % 2][:, c * P:(c + 1) * P], xb[n][:, c, 0:D], ident[:])
                    ins.then_inc(s["blk_tp"], 1)
                if from_on(b, 1) and (not isinstance(b, int) or b - 1 < NB):
                    m = (n - 1) % NBUF
                    pe.wait_ge(wb_in[m], 16 * turn(1) + 16)
                    pe.wait_ge(s["blk_tr"], b)
                    if from_on(b, 3):
                        pe.wait_ge(s["blk_gelu"], b - 2)
                    pe.wait_ge(s["blk_wlo"], b)
                    for c in range(CH):
                        w = [part[m % 2][:, c * P:(c + 1) * P] for part in (w_hi, w_lo)]
                        h = blk_h[m % 2][c // 2][:, (c % 2) * BLK:(c % 2 + 1) * BLK]
                        t.matmul(h, w[0], x_lo[m % 2][:], start=True, stop=False)
                        t.matmul(h, w[0], x_hi[m % 2][:], start=False, stop=False)
                        ins = t.matmul(h, w[1], x_hi[m % 2][:], start=False, stop=True)
                    ins.then_inc(s["blk_fc"], 1)
                if from_on(b, 2):
                    m = (n - 2) % NBUF
                    pe.wait_ge(s["blk_gelu"], b - 1)
                    if from_on(b, 4):
                        pe.wait_ge(s["blk_yr"], b - 3)
                    for c in range(CH):
                        for r in range(2):
                            ins = t.matmul(blk_y[m % 2][:, r * D:(r + 1) * D], hb[m % 2][:, c, r * P:(r + 1) * P],
                                           wb[m][:, HID + c * D:HID + (c + 1) * D],
                                           start=(c == 0 and r == 0), stop=True, skip_group_check=True)
                    ins.then_inc(s["blk_mm2"], 1)

            over_blocks(pe, step, extra=2)

        @block.vector
        def _(dve):
            v = nc.vector
            def stats(which, src, count):
                for j in range(TILES):
                    ins = v.bn_stats(bst[:, which, j], src(j))
                ins.then_inc(s[f"ln{which}_st"], 1)
                dve.wait_ge(s[f"ln{which}_st"], count)
                alone(dve)
                for j in range(TILES):
                    ins = v.bn_aggr(mv[:, which, j], bst[:, which, j])
                ins.then_inc(s[f"ln{which}_mv"], 1)

            def ln0_stats(st):
                stats(0, lambda j: Xt(st, j), st + 1)

            dve.wait_ge(s["x_first"], 16)
            ln0_stats(0)
            dve.wait_ge(s["consts"], 4)
            dve.wait_ge(s["bias_in"], 48)
            v.tensor_copy(bqkv_rows[:], bqkv_raw[:].rearrange("r (h e) -> r e h", h=H)
                          ).then_inc(s["setup_dve"], 1)
            v.tensor_reduce(head_ones[:], ident[:].rearrange("p (e h) -> p h e", e=E), AX_X, ALU.add)
            dve.wait_ge(s["w_first"], 32)
            for m in range(3):
                ins = v.tensor_copy(wqkv_sb[:, m], wqkv_raw[:, m * D:(m + 1) * D].rearrange("p (h e) -> p e h", h=H))
            ins.then_inc(s["setup_dve"], 1)
            dve.wait_ge(s["setup_pe"], 1)
            v.tensor_copy(bias_cols[:], bS[:, 0:NBIAS])
            v.tensor_copy(bk_col[:], bS[:, 65:66])
            v.tensor_scalar(bq_scaled[:], bS[:, 64:65], E ** -0.5, None, ALU.mult).then_inc(s["setup_dve"], 1)
            dve.wait_ge(s["setup_dve"], 3)
            v.tensor_copy(b12[:, :, 0:CH], bias_cols[:, 0:NE * CH].rearrange("p (e c) -> p e c", e=NE))
            dve.wait_ge(s["setup_pe"], 2)
            for half in range(2):
                ins = v.tensor_copy(wout_t[:, half], bO[:, 0:D].rearrange("p (h e) -> p e h", h=H))
            ins.then_inc(s["setup_dve"], 1)

            dve.wait_ge(s["rows_in"], 48)
            v.tensor_copy(bias_f[:, 0].rearrange("p (e h) -> p e h", e=E),
                          bias_raw[:, 0].rearrange("p (h e) -> p e h", h=H))
            v.tensor_copy(bias_f[:, 1:3], bias_raw[:, 1:3]).then_inc(s["bias_parts"], 1)
            for n in range(3):
                v.memset(ones3[32 * n:32 * n + 1, :], 1.0)
                dve.wait_ge(s["bias_parts"], 2 * n + 1)
                v.tensor_copy(bias_part[n][:], bias_f[:]).then_inc(s["bias_parts"], 1)
                dve.wait_ge(s["bias_parts"], 2 * n + 2)
                ins = v.tensor_copy(bias3[32 * n:32 * n + 1], bias_part[n][32 * n:32 * n + 1])
                if n < 2:
                    ins = v.tensor_tensor(bias_f[:], bias_f[:], bias_part[n][:], ALU.subtract)
                ins.then_inc(s["bias_parts"], 1)

            dve.wait_ge(s["setup_pe"], 3)
            for half in range(2):
                ins = v.tensor_copy(wout_rot[:, 4 * half:4 * half + 4],
                                    bV[half][:].rearrange("p (a d) -> p a d", a=4))
            ins.then_inc(s["setup_dve"], 1)
            dve.wait_ge(s["x_rest"], 32)

            def prod(i, d):
                dve.wait_ge(s["vt_done"], E * i + d + 1)
                v.scalar_tensor_tensor(out=KV[:, d], in0=qk0[:, 1], scalar=FEAT_EPS, in1=bV[d % 2][:],
                                       op0=ALU.add, op1=ALU.mult).then_inc(s["kv_prod"], 1)

            def sums(i, part):
                dve.wait_ge(s["kv_prod"], E * i + 2 * part + 2)
                w = KV[:, 2 * part:2 * part + 2].rearrange("p a t -> p (a t)")
                v.tensor_tensor_scan(w, keep[:], w, 0.0, ALU.mult, ALU.add).then_inc(s["kv_sum"], 1)

            def zed(i, part):
                dve.wait_ge(s["kv_sum"], 4 * i + part + 1)
                v.tensor_tensor(Z[:, 2 * part:2 * part + 2], KV[:, 2 * part:2 * part + 2],
                                qn[:].unsqueeze(1).broadcast_to([P, 2, STEP]), ALU.mult).then_inc(s["z_ready"], 1)

            def route_top(i):
                dve.wait_ge(s["lg_done"], i - 1)
                v.tensor_copy(lg[:], ps_lg.rearrange("p (t e) -> p t e", t=TILES)).then_inc(s["lg_read"], 1)
                dve.wait_ge(s["lg_read"], i - 1)
                alone(dve)
                for j in range(TILES):
                    v.max(top[:, j], lg[:, j]).then_inc(s["top_ready"], 1)
                for j in range(TILES):
                    dve.wait_ge(s["top_ready"], 2 * TILES * (i - 2) + j + 1)
                    alone(dve)
                    v.max_index(topi[:, j], top[:, j], lg[:, j]).then_inc(s["top_ready"], 1)
                g = gap[:, bass.ds(TILES * (i - 2), TILES)]
                v.tensor_tensor(g, top[:, :, 1], top[:, :, 0], ALU.subtract)
                dve.wait_ge(s["top_ready"], 2 * TILES * (i - 1))
                v.tensor_copy(idxf[:], topi[:, :, 0:2].rearrange("p t k -> p k t")
                              ).then_inc(s["idx_ready"], 1)

            def route_hot(i):
                dve.wait_ge(s["idx_ready"], i - 1)
                v.tensor_tensor(onehot[:].rearrange("p k t e -> p (k t) e"),
                                idxf[:].rearrange("p k t -> p (k t)").unsqueeze(2)
                                .broadcast_to([P, 2 * TILES, NE]),
                                iota8[:].unsqueeze(1).broadcast_to([P, 2 * TILES, NE]),
                                ALU.is_equal).then_inc(s["hot_ready"], 1)

            def route_chosen(i):
                dve.wait_ge(s["hot_ready"], i - 1)
                if from_on(i, 3):
                    dve.wait_ge(s["rank_done"], i - 2)
                v.tensor_tensor(chosen[:], onehot[:, 0], onehot[:, 1], ALU.add).then_inc(s["chosen_ready"], 1)

            def route_sum(i):
                dve.wait_ge(s["chosen_ready"], i - 1)
                v.tensor_reduce(chosen_sum[:], chosen[:].rearrange("p t e -> p e t"), AX_X,
                                ALU.add).then_inc(s["acc_red"], 1)

            def route_place(i):
                dve.wait_ge(s["rank_done"], i - 1)
                v.tensor_tensor(place[:], ps_rank.rearrange("p (t e) -> p t e", t=TILES),
                                list_base[:].unsqueeze(1).broadcast_to([P, TILES, NE]),
                                ALU.add).then_inc(s["place_ready"], 1)
                dve.wait_ge(s["acc_red"], i - 1)
                v.tensor_tensor(chosen_acc[:], chosen_acc[:], chosen_sum[:], ALU.add
                                ).then_inc(s["acc_ready"], 1)
                dve.wait_ge(s["place_ready"], i - 1)
                v.tensor_tensor(placed[:], onehot[:], place[:].unsqueeze(1).broadcast_to([P, 2, TILES, NE]),
                                ALU.mult).then_inc(s["placed_ready"], 1)

            def route_pos(i):
                dve.wait_ge(s["placed_ready"], i - 1)
                v.tensor_reduce(posf[:], placed[:].rearrange("p k t e -> p (k t) e"), AX_X,
                                ALU.add).then_inc(s["posf_ready"], 1)
                if from_on(i, 3):
                    dve.wait_ge(s["scattered"], 16 * 2 * TILES * (i - 2))
                dst = dest[:, i - 2] if isinstance(i, int) else \
                    dest[:, bass.ds(i - 2, 1)].rearrange("p o k t -> p (o k) t")
                v.tensor_copy(rows[:].bitcast(I32)[:, :, :, D:ROW].rearrange("p k t o -> p k (t o)"),
                              dst).then_inc(s["dest_ready"], 1)
                dve.wait_ge(s["posf_ready"], i - 1)
                v.tensor_copy(pos[:], posf[:]).then_inc(s["pos_ready"], 1)

            def route(i):
                for part in (route_top, route_hot, route_chosen, route_sum, route_place, route_pos):
                    part(i)

            def iteration(i, head, tail, nxt, routed):
                again = from_on(i, 1)
                if not head:
                    route(i)
                    routed = False
                if head:
                    dve.wait_ge(s["qk_read"], i + 1)
                    if again:
                        dve.wait_ge(s["k1_ready"], i)
                    v.scalar_tensor_tensor(out=qk0[:], in0=e_qk[:], scalar=1.0, in1=r_qk[:], op0=ALU.min,
                                           op1=ALU.add).then_inc(s["qk_ready"], 1)
                    dve.wait_ge(s["qk_ready"], i + 1)
                    prod(i, 0)
                    prod(i, 1)
                if nxt:
                    ln0_stats(i + 1)
                if head:
                    dve.wait_ge(s["k1_ready"], i + 1)
                    v.tensor_tensor_scan(KC[:], keep[:, 0:STEP], k1[:], 0.0, ALU.mult,
                                         ALU.add).then_inc(s["kc_ready"], 1)
                    dve.wait_ge(s["kc_ready"], i + 1)
                    if again:
                        dve.wait_ge(s["den_done"], i)
                    v.scalar_tensor_tensor(out=pden[:], in0=qk0[:, 0], scalar=FEAT_EPS, in1=KC[:], op0=ALU.add,
                                           op1=ALU.mult).then_inc(s["p_ready"], 1)
                    prod(i, 2)
                    prod(i, 3)
                if tail:
                    dve.wait_ge(s["out_done"], i)
                    stats(1, lambda j: bO[:, j * D:(j + 1) * D], i)
                if routed:
                    route_top(i)
                if head:
                    sums(i, 0)
                if routed:
                    route_hot(i)
                if head:
                    dve.wait_ge(s["den_done"], i + 1)
                    v.tensor_scalar(den[:], ps_den, DEN_EPS, None, ALU.add).then_inc(s["den_add"], 1)
                    prod(i, 4)
                if routed:
                    route_chosen(i)
                if head:
                    dve.wait_ge(s["den_add"], i + 1)
                    v.reciprocal(rden[:].rearrange("p t h -> p (t h)"), den[:]).then_inc(s["den_inv"], 1)
                    prod(i, 5)
                    dve.wait_ge(s["den_inv"], i + 1)
                    if again:
                        dve.wait_ge(s["exp_done"], i)
                    for j in range(TILES):
                        ins = v.tensor_copy(rden8[:, j], rden[:, j].unsqueeze(1).broadcast_to([P, E, H]))
                    ins.then_inc(s["rden_ready"], 1)
                if head:
                    sums(i, 1)
                if routed:
                    route_sum(i)
                if tail:
                    dve.wait_ge(s["x1_ready"], i)
                    stats(2, lambda j: Xt(i - 1, j), i)
                if routed:
                    route_place(i)
                if head:
                    prod(i, 6)
                    dve.wait_ge(s["exp_done"], i + 1)
                    v.scalar_tensor_tensor(out=qn[:], in0=qk0[:, 0], scalar=FEAT_EPS, in1=bB[:], op0=ALU.add,
                                           op1=ALU.mult).then_inc(s["qn_ready"], 1)
                    prod(i, 7)
                if routed:
                    route_pos(i)
                if head:
                    sums(i, 2)
                    dve.wait_ge(s["qn_ready"], i + 1)
                    if again:
                        dve.wait_ge(s["out_done"], i)
                    zed(i, 0)
                    sums(i, 3)
                    for part in range(1, 4):
                        zed(i, part)

            all_iterations(dve, iteration)

            n = [0]

            def link(ins):
                n[0] += 1
                ins.then_inc(s["tab"], 1)
                dve.wait_ge(s["tab"], n[0])

            M = LIST // BLK - 1
            dve.wait_ge(s["cnt_done"], 1)
            link(v.tensor_copy(cnt[:], bS[0:1, 0:NE]))
            link(v.tensor_tensor(tabf[:, 2 * NB:2 * NB + NE], cnt[:], list_base[0:1, :], ALU.add))
            v.tensor_copy(ends[:], tabf[:, 2 * NB:2 * NB + NE]).then_inc(s["ends_ready"], 1)
            link(v.tensor_tensor(full16[:], cnt[:].unsqueeze(2).broadcast_to([1, NE, M]), steps16[:], ALU.is_gt))
            link(v.tensor_reduce(nblk[:], full16[:], AX_X, ALU.add))
            link(v.tensor_tensor_scan(cum[:], one8[:], nblk[:], 0.0, ALU.mult, ALU.add))
            link(v.tensor_scalar(jump[:], nblk[:], -float(BLK), float(LIST), ALU.mult, ALU.add))
            link(v.tensor_tensor(past[:], bnum[:], cum[:].unsqueeze(1).broadcast_to([1, NB, NE]), ALU.is_ge))
            link(v.tensor_reduce(tabf[:, 0:NB], past[:], AX_X, ALU.add))
            link(v.tensor_scalar(tabf[:, 0:NB], tabf[:, 0:NB], float(NE - 1), None, ALU.min))
            link(v.tensor_tensor(pastj[:], past[:], jump[:].unsqueeze(1).broadcast_to([1, NB, NE]), ALU.mult))
            link(v.tensor_reduce(tabf[:, NB:2 * NB], pastj[:], AX_X, ALU.add))
            link(v.tensor_tensor(tabf[:, NB:2 * NB], tabf[:, NB:2 * NB], b256[:], ALU.add))
            v.tensor_copy(table[:], tabf[:, 0:2 * NB]).then_inc(s["table_ready"], 1)

            def step(b, n, turn):
                if not isinstance(b, int) or b < NB:
                    dve.wait_ge(s["blk_tp"], b + 1)
                    if from_on(b, 2):
                        dve.wait_ge(s["blk_fc"], b - 1)
                    v.tensor_copy(x_hi[n % 2][:], blk_t[n % 2]).then_inc(s["blk_xhi"], 1)
                    dve.wait_ge(s["blk_whi"], b + 1)
                    v.tensor_tensor(w_lo[n % 2][:], wb[n][:, 0:HID], w_hi[n % 2][:].bitcast(F32), ALU.subtract
                                    ).then_inc(s["blk_wlo"], 1)
                    dve.wait_ge(s["blk_xhi"], b + 1)
                    v.tensor_tensor(x_lo[n % 2][:], blk_t[n % 2], x_hi[n % 2][:].bitcast(F32), ALU.subtract
                                    ).then_inc(s["blk_tr"], 1)
                if from_on(b, 2):
                    m = (n - 2) % NBUF
                    dve.wait_ge(s["blk_mm2"], b - 1)
                    if from_on(b, NBUF + 2):
                        dve.wait_ge(blk_scat[m], 32 * turn(2))
                    v.tensor_tensor(yb[m][:], blk_y[m % 2][:, 0:2 * D].rearrange("p (r d) -> p r d", r=2),
                                    wb[m][:, B2_AT:WROW].unsqueeze(1).broadcast_to([P, 2, D]),
                                    ALU.add).then_inc(s["blk_yr"], 1)

            over_blocks(dve, step, extra=2)

            dve.wait_ge(s["gate_exp"], 1)
            v.tensor_scalar(gates[:, 0], gates[:, 1], 1.0, None, ALU.add).then_inc(s["gate_w"], 1)
            dve.wait_ge(s["gate_w"], 1)
            v.reciprocal(gates[:, 0], gates[:, 0]).then_inc(s["gate_w"], 1)
            dve.wait_ge(s["gate_w"], 2)
            v.tensor_tensor(gates[:, 1], gates[:, 1], gates[:, 0], ALU.mult).then_inc(s["gate_w"], 1)
            dve.wait_ge(s["gate_w"], 3)

            for g in range(NS):
                y, m = Y[g // PER_Y][:, g % PER_Y], g % 3
                dve.wait_ge(y_in[g], 16)
                for k, done in enumerate(("fin_y0", "fin_y1")):
                    for j in range(TILES):
                        n = TILES * g + j
                        ins = v.scalar_tensor_tensor(out=SH[:, n], in0=y[:, j, k], scalar=gates[:, k, n:n + 1],
                                                     in1=SH[:, n], op0=ALU.mult, op1=ALU.add)
                    ins.then_inc(s[done], 1)
                    dve.wait_ge(s[done], g + 1)
                for j in range(TILES):
                    ins = v.bn_stats(bst[:, m, j], SH[:, TILES * g + j])
                ins.then_inc(s["fin_st"], 1)
                dve.wait_ge(s["fin_st"], g + 1)
                if g >= 3:
                    dve.wait_ge(s["fin_shift"], g - 2)
                for j in range(TILES):
                    ins = v.bn_aggr(mv[:, m, j], bst[:, m, j])
                ins.then_inc(s["fin_mv"], 1)


_INS = ['L0_attn_x', 'L0_attn_W_qkv', 'L0_attn_b_qkv', 'L0_attn_W_out', 'L0_attn_b_out', 'L0_ffn_Wfc_s',
        'L0_ffn_bfc_s', 'L0_ffn_Wproj_s', 'L0_ffn_bproj_s', 'L0_ffn_Wr', 'L0_ffn_Wfc', 'L0_ffn_bfc',
        'L0_ffn_Wproj', 'L0_ffn_bproj']


def kernel(**inputs):
    import numpy as _np
    import concourse.bacc as _bacc
    from concourse import mybir as _mybir
    from concourse.bass_utils import run_bass_kernel_spmd as _run

    nc = _bacc.Bacc("TRN2", target_bir_lowering=False, num_devices=1)
    arrays, args = {}, []
    for name in _INS:
        a = _np.ascontiguousarray(inputs[name])
        arrays[f"in_{name}"] = a
        args.append(nc.dram_tensor(f"in_{name}", a.shape, _mybir.dt.from_np(a.dtype), kind="ExternalInput").ap())
    shape = inputs['L0_attn_x'].shape
    args.append(nc.dram_tensor("out_0", shape, _mybir.dt.float32, kind="ExternalOutput").ap())
    sandwich_kernel(nc, *args)
    r = _run(nc, [arrays], core_ids=[0])
    return r.results[0]["out_0"]
```

```python
from contextlib import ExitStack

import concourse.bass as bass
from concourse import mybir

ALU = mybir.AluOpType
ACT = mybir.ActivationFunctionType
F32 = mybir.dt.float32
BF16 = mybir.dt.bfloat16
F32R = mybir.dt.float32r
I32 = mybir.dt.int32
U32 = mybir.dt.uint32
AX_X = mybir.AxisListType.X

P = 128
D = 128
H, E = 16, 8
L = 256
TILES = 4
STEP = TILES * P
HID = 512
CH = HID // P
NE = 8
BLK = 256
FEAT_EPS = 1e-4
DEN_EPS = 1e-6
LN_EPS = 1e-5


def sandwich_kernel(nc, x, w_qkv, b_qkv, w_out, b_out, wfc_s, bfc_s, wproj_s, bproj_s, wr, wfc, bfc, wproj,
                    bproj, out):
    x_rows = x.rearrange("b l d -> (b l) d")
    out_rows = out.rearrange("b l d -> (b l) d")
    TOKENS = x_rows.shape[0]
    NS = TOKENS // STEP
    NT = TOKENS // P
    PAIRS = 2 * TOKENS
    NB = PAIRS // BLK + NE - 1
    SPARE = NB - PAIRS // BLK
    EARLY = -(-(PAIRS - 2 * STEP - NE * (BLK - 1)) // BLK)
    LIST = TOKENS + BLK
    ROW = D + 1
    WROW = HID + CH * D + CH + D
    B1_AT = HID + CH * D
    B2_AT = B1_AT + CH
    PADS = NE + SPARE
    NBUF = 6
    CLOSED = 2 * NBUF - 1
    assert NE <= CLOSED + 1 <= EARLY

    lists = nc.dram_tensor("expert_lists", [NE * LIST + SPARE * BLK, ROW], F32).ap()
    results = nc.dram_tensor("expert_results", [PAIRS + PADS * BLK, D], F32).ap()
    packed = nc.dram_tensor("packed_weights", [NE, P, WROW], F32).ap()

    with ExitStack() as ctx:
        def sb(name, shape, dt=F32):
            return ctx.enter_context(nc.sbuf_tensor(name, shape, dt))

        def bank(name, shape, dt=F32):
            return ctx.enter_context(nc.psum_tensor(name, shape, dt))

        def sem(name):
            return ctx.enter_context(nc.semaphore(name))

        ident = sb("ident", [P, P])
        ones3 = sb("ones3", [P, P], BF16)
        head_ones = sb("head_ones", [P, H])
        before = sb("before", [P, P], BF16)
        ones_bf = sb("ones_bf", [P, P], BF16)
        keep = sb("keep", [P, 2 * STEP], BF16)
        iota8 = sb("iota8", [P, NE])
        list_base = sb("list_base", [P, NE])
        dest = sb("dest", [P, NS, 2, TILES], I32)
        neg_half = sb("neg_half", [P, TILES])
        ln_eps = sb("ln_eps", [P, TILES])
        minus_one = sb("minus_one", [P, TILES])
        wqkv_raw = sb("wqkv_raw", [P, 3 * D])
        wqkv_sb = sb("wqkv_sb", [P, 3, E, H])
        wout_sb = sb("wout_sb", [P, D])
        wout_t = sb("wout_t", [P, 2, E, H])
        wout_rot = sb("wout_rot", [P, E, D])
        wr_sb = sb("wr_sb", [P, NE])
        w1s_sb = sb("w1s_sb", [P, HID])
        w2s_sb = sb("w2s_sb", [P, CH, D])
        NBIAS = NE * CH + CH
        bias_rows = sb("bias_rows", [NBIAS, P])
        bias_cols = sb("bias_cols", [P, NBIAS])
        bqkv_raw = sb("bqkv_raw", [3, D])
        bqkv_rows = sb("bqkv_rows", [3, E, H])
        bq_scaled = sb("bq_scaled", [P, 1])
        bk_col = sb("bk_col", [P, 1])
        bias_raw = sb("bias_raw", [P, 3, D])
        bias_f = sb("bias_f", [P, 3, D])
        bias_part = [sb(f"bias_part{n}", [P, 3, D], BF16) for n in range(3)]
        bias3 = sb("bias3", [P, 3, D], BF16)
        b12 = sb("b12", [P, NE, CH + D])
        pads = sb("pads", [P, PADS, 2, ROW])
        X = sb("X", [P, NT, D])
        SH = sb("SH", [P, NT, D])
        bst = sb("bst", [P, 3, TILES, 6])
        mv = sb("mv", [P, 3, TILES, 2])
        ve = sb("ve", [P, 3, TILES])
        rstd = sb("rstd", [P, 3, TILES])
        neg_mean = sb("neg_mean", [P, 3, TILES])
        shift = sb("shift", [P, 3, TILES])
        xn = sb("xn", [P, TILES, D])
        xn_t = sb("xn_t", [P, STEP])
        e_qk = sb("e_qk", [P, 2, STEP])
        r_qk = sb("r_qk", [P, 2, STEP])
        qk0 = sb("qk0", [P, 2, STEP])
        k1 = sb("k1", [P, STEP])
        vdup = sb("vdup", [P, TILES, 2 * D])
        KV = sb("KV", [P, E, STEP])
        KC = sb("KC", [P, STEP])
        pden = sb("pden", [P, STEP])
        den = sb("den", [P, TILES * H])
        rden = sb("rden", [P, TILES, H])
        rden8 = sb("rden8", [P, TILES, E, H])
        qn = sb("qn", [P, STEP])
        Z = sb("Z", [P, E, STEP])
        attn = sb("attn", [P, TILES, D])
        rows = sb("rows", [P, 2, TILES, ROW])
        xn2 = sb("xn2", [P, TILES, D])
        xt2 = sb("xt2", [P, STEP])
        hs = sb("hs", [P, CH, STEP])
        w_hi = [sb(f"w_hi{n}", [P, HID], F32R) for n in range(2)]
        w_lo = [sb(f"w_lo{n}", [P, HID], F32R) for n in range(2)]
        w1s_hi, w1s_lo, xt2_hi, xt2_lo = w_hi[0], w_lo[0], w_hi[1], w_lo[1]
        lg = sb("lg", [P, TILES, NE])
        top = sb("top", [P, TILES, 8])
        topi = sb("topi", [P, TILES, 8], U32)
        idxf = sb("idxf", [P, 2, TILES])
        onehot = sb("onehot", [P, 2, TILES, NE])
        chosen = sb("chosen", [P, TILES, NE], BF16)
        chosen_sum = sb("chosen_sum", [P, NE])
        chosen_acc = sb("chosen_acc", [P, NE], BF16)
        gap = sb("gap", [P, NT])
        place = sb("place", [P, TILES, NE])
        placed = sb("placed", [P, 2, TILES, NE])
        posf = sb("posf", [P, 2 * TILES])
        pos = sb("pos", [P, 2 * TILES], I32)
        gates = sb("gates", [P, 2, NT])
        cnt = sb("cnt", [1, NE])
        steps16 = sb("steps16", [1, NE, LIST // BLK - 1])
        full16 = sb("full16", [1, NE, LIST // BLK - 1])
        nblk = sb("nblk", [1, NE])
        cum = sb("cum", [1, NE])
        warm = sb("warm", [1, NE])
        cum_done = sb("cum_done", [1, NE + 1])
        done = sb("done", [1, NE + 1])
        first_row = sb("first_row", [1, 1])
        step_up = sb("step_up", [1, NE])
        one8 = sb("one8", [1, NE])
        jump = sb("jump", [1, NE])
        bnum = sb("bnum", [1, NB, NE])
        past = sb("past", [1, NB, NE])
        pastj = sb("pastj", [1, NB, NE])
        b256 = sb("b256", [1, NB])
        tabf = sb("tabf", [1, 2 * NB + NE])
        table = sb("table", [1, 2 * NB], I32)
        ends = sb("ends", [1, NE], I32)
        kvz = [w[:].rearrange("p a t -> p (a t)") for w in (KV, Z)]
        wb = [kvz[n // 3][:, (n % 3) * WROW:(n % 3 + 1) * WROW] for n in range(NBUF)]
        xb = [sb(f"xb{n}", [P, 2, ROW]) for n in range(NBUF)]
        x_hi = [sb(f"x_hi{n}", [P, BLK], F32R) for n in range(2)]
        x_lo = [sb(f"x_lo{n}", [P, BLK], F32R) for n in range(2)]
        hb = [hs[:].rearrange("p c (n t) -> p n c t", n=2)[:, n] for n in range(2)]
        yb = [sb(f"yb{n}", [P, 2, D]) for n in range(NBUF)]
        Y = [w.rearrange("p (n t k d) -> p n t k d", t=TILES, k=2, d=D) for w in kvz]
        PER_Y = Y[0].shape[1]

        bT = bank("bT", [P, STEP])
        bA = bank("bA", [P, STEP])
        bB = bank("bB", [P, STEP])
        bV = [bank(f"bV{n}", [P, STEP]) for n in range(2)]
        bO = bank("bO", [P, STEP])
        bS = bank("bS", [P, STEP])
        bH = bank("bH", [P, STEP])
        ps_den, ps_lg, ps_rank = bB[:, 0:TILES * H], bS[:, 64:64 + TILES * NE], bS[:, 128:128 + TILES * NE]
        blk_t = [bT[:, 0:BLK], bH[:, 0:BLK]]
        blk_h = [[bA, bB], [bV[0], bV[1]]]
        blk_y = [bO, bS]

        names = """waited x_first x_second x_rest w_first w_rest bias_in rows_in b2_in bias_parts packed_w packed_b
            consts setup_pe setup_dve
            ln0_mv ln0_rstd xn_ready t0_done xnt_ready q_mm k_mm v_mm q_read qk_read vdup_ready qk_ready k1_ready
            vt_done kv_prod kc_ready kv_sum p_ready den_done den_add den_inv rden_ready exp_done qn_ready z_ready z1_ready out_done
            ln1_st ln1_mv ve0_ready ve1_ready ve2_ready pow0_done pow1_done pow2_done ln1_rstd attn_ready x1_ready ln2_st ln2_mv ln2_rstd ln0_st
            xn2_ready dest_ready rows_ready t2_done xt2_ready
            fc_done w1s_hi w1s_lo xt2_lo gelu_done sh_done sh_read
            lg_done lg_read top_ready idx_ready hot_ready hot_both chosen_ready rank_done acc_red acc_ready
            place_ready placed_ready posf_ready pos_ready scattered
            pads_ready spare_in cnt_done cnt_read tab table_ready ends_ready tails_in
            blk_tp blk_xhi blk_whi blk_wlo blk_tr blk_fc blk_gelu blk_mm2 blk_yr
            gate_exp gate_w fin_scaled fin_y0 fin_y1 fin_st fin_mv fin_ve fin_pow fin_shift fin_n fin_done out_stored""".split()
        s = {n: sem(n) for n in names}
        wb_in = [sem(f"wb_in{n}") for n in range(NBUF)]
        xb_in = [sem(f"xb_in{n}") for n in range(NBUF)]
        blk_scat = [sem(f"blk_scat{n}") for n in range(NBUF)]
        y_in = [sem(f"y_in{n}") for n in range(NS)]
        block = ctx.enter_context(nc.Block())

        def alone(eng):
            eng.sem_inc(s["waited"], 1)

        def over_blocks(eng, step, extra=0, first=1):
            def one(b, n, t):
                step(b, n, lambda k: t - (k > n))

            for b in range(first * NBUF):
                one(b, b % NBUF, b // NBUF)
            with eng.Fori(first, NB // NBUF) as t:
                for n in range(NBUF):
                    one(t * NBUF + n, n, t)
            for b in range(NB - NB % NBUF, NB + extra):
                one(b, b % NBUF, b // NBUF)

        def Xt(st, j):
            if isinstance(st, int):
                return X[:, TILES * st + j, :]
            return X[:, bass.ds(TILES * st + j, 1), :].rearrange("p o d -> p (o d)")

        def all_iterations(eng, iteration):
            iteration(0, True, False, True, False)
            iteration(1, True, True, True, False)
            iteration(2, True, True, True, True)
            with eng.Fori(3, NS - 1) as i:
                iteration(i, True, True, True, True)
            iteration(NS - 1, True, True, False, True)
            iteration(NS, False, True, False, True)
            iteration(NS + 1, False, False, False, True)

        def from_on(b, first):
            return not isinstance(b, int) or b >= first

        def store(sp, g):
            sp.wait_ge(s["fin_done"], g + 1)
            sp.dma_start(out_rows[g * STEP:(g + 1) * STEP, :].rearrange("(t p) d -> p t d", p=P),
                         SH[:, TILES * g:TILES * (g + 1)]).then_inc(s["out_stored"], 16)

        @block.sync
        def _(sp):
            def xt(a, b):
                return x_rows[a * P:b * P, :].rearrange("(t p) d -> p t d", p=P)

            sp.dma_start(X[:, 0:TILES, :], xt(0, TILES)).then_inc(s["x_first"], 16)
            n = NE * CH
            sp.dma_start(bias_rows[0:n, :], bfc.rearrange("e (c p) -> (e c) p", p=P)).then_inc(s["bias_in"], 16)
            sp.dma_start(bias_rows[n:n + CH, :], bfc_s.rearrange("(c p) -> c p", p=P)).then_inc(s["bias_in"], 16)
            sp.dma_start(X[:, TILES:2 * TILES, :], xt(TILES, 2 * TILES)).then_inc(s["x_second"], 16)
            sp.wait_ge(s["consts"], 1)
            for k, src in enumerate((b_qkv[2 * D:3 * D], b_out, bproj_s)):
                sp.dma_start(bias_raw[0:96:32, k],
                             src.rearrange("(o d) -> o d", o=1).broadcast_to([3, D])).then_inc(s["rows_in"], 16)
            sp.dma_start(wr_sb[:], wr).then_inc(s["w_rest"], 16)
            sp.dma_start(w1s_sb[:], wfc_s).then_inc(s["w_rest"], 16)
            sp.dma_start(w2s_sb[:], wproj_s.rearrange("(c p) n -> p c n", p=P)).then_inc(s["w_rest"], 16)
            sp.dma_start(X[:, 2 * TILES:NT, :], xt(2 * TILES, NT)).then_inc(s["x_rest"], 16)
            sp.dma_start(b12[:, :, CH:CH + D], bproj.rearrange("(o e) d -> o e d", o=1).broadcast_to([P, NE, D])
                         ).then_inc(s["b2_in"], 16)
            for e in range(NE):
                sp.dma_start(packed[e, :, 0:HID], wfc[e]).then_inc(s["packed_w"], 16)
                sp.dma_start(packed[e, :, HID:B1_AT].rearrange("p (c n) -> p c n", c=CH),
                             wproj[e].rearrange("(c p) n -> p c n", p=P)).then_inc(s["packed_w"], 16)
            sp.wait_ge(s["b2_in"], 16)
            sp.wait_ge(s["setup_dve"], 4)
            sp.dma_start(packed[:, :, B1_AT:WROW].rearrange("e p n -> p e n"), b12[:]).then_inc(s["packed_b"], 16)
            sp.wait_ge(s["pads_ready"], 2)
            sp.dma_start(lists[NE * LIST:, :].rearrange("(c p) n -> p c n", p=P),
                         pads[:, NE:PADS, :, :].rearrange("p a c n -> p (a c) n")).then_inc(s["spare_in"], 16)
            sp.wait_ge(s["spare_in"], 16)
            sp.wait_ge(s["table_ready"], 1)
            sp.wait_ge(s["packed_w"], 16 * 2 * NE)
            sp.wait_ge(s["packed_b"], 16)

            def close_list(e):
                if e == 0:
                    sp.wait_ge(s["ends_ready"], 1)
                at = sp.value_load(ends[0:1, e:e + 1], min_val=e * LIST, max_val=e * LIST + TOKENS)
                sp.dma_start(lists[bass.ds(at, BLK), :].rearrange("(c p) n -> p c n", p=P),
                             pads[:, e, :, :]).then_inc(s["tails_in"], 16)

            def lists_closed():
                sp.wait_ge(s["tails_in"], 16 * NE)
                sp.wait_ge(s["scattered"], 16 * 2 * NT)
                sp.wait_ge(s["table_ready"], 2)

            def load_block(b, n, turn):
                who = sp.value_load(table[0:1, bass.ds(b, 1)], min_val=0, max_val=NE - 1)
                at = sp.value_load(table[0:1, bass.ds(b + NB, 1)], min_val=0,
                                   max_val=NE * LIST + (SPARE - 1) * BLK)
                if from_on(b, NBUF):
                    sp.wait_ge(s["blk_yr"], b - NBUF + 1)
                    alone(sp)
                sp.dma_start(wb[n], packed[bass.ds(who, 1), :, :].rearrange("e p n -> p (e n)")
                             ).then_inc(wb_in[n], 16)
                if isinstance(b, int) and b == 0:
                    sp.wait_ge(s["scattered"], 16 * 2 * (NT - TILES))
                if from_on(b, NBUF):
                    sp.wait_ge(blk_scat[n], 32 * turn(0))
                    alone(sp)
                sp.dma_start(xb[n][:], lists[bass.ds(at, BLK), :].rearrange("(c p) n -> p c n", p=P)
                             ).then_inc(xb_in[n], 16)
                if isinstance(b, int) and CLOSED - NE < b <= CLOSED:
                    close_list(b - 1 - CLOSED + NE)
                if isinstance(b, int) and b == CLOSED:
                    lists_closed()

            over_blocks(sp, load_block, first=2)
            for n in range(NBUF):
                sp.wait_ge(blk_scat[n], 32 * ((NB - n + NBUF - 1) // NBUF))
            for g in range(NS):
                sp.dma_start(Y[g // PER_Y][:, g % PER_Y].rearrange("p t k d -> p t (k d)"),
                             results[2 * g * STEP:2 * (g + 1) * STEP, :]
                             .rearrange("(t p k) d -> p t (k d)", p=P, k=2)).then_inc(y_in[g], 16)
            for g in range(NS):
                store(sp, g)
            sp.wait_ge(s["out_stored"], 16 * NS)

        @block.gpsimd
        def _(pool):
            g = nc.gpsimd
            g.memset(bias_raw[:], 0.0).then_inc(s["consts"], 1)
            g.memset(bias3[:], 0.0)
            g.memset(ones3[:], 0.0)
            g.memset(ident[:], 0.0)
            g.memset(before[:], 1.0)
            g.memset(ones_bf[:], 1.0)
            g.memset(keep[:], 1.0)
            g.memset(neg_half[:], -0.5)
            g.memset(ln_eps[:], LN_EPS)
            g.memset(minus_one[:], -1.0)
            g.memset(chosen_acc[:], 0.0)
            g.memset(cum_done[:], 0.0)
            g.memset(done[:], 0.0)
            g.memset(one8[:], 1.0).then_inc(s["consts"], 1)
            pool.wait_ge(s["consts"], 2)
            g.affine_select(out=ident[:], in_=ident[:], compare_op=ALU.not_equal, fill=1.0, base=0,
                            pattern=[[-1, P]], channel_multiplier=1)
            g.memset(keep[:].rearrange("p (a b) -> p a b", b=L)[:, :, 0:1], 0.0)
            g.affine_select(out=before[:], in_=before[:], compare_op=ALU.is_gt, fill=0.0, base=0,
                            pattern=[[1, P]], channel_multiplier=-1).then_inc(s["consts"], 1)

            def inv_std(which, count):
                pool.wait_ge(s[f"ln{which}_mv"], count)
                g.tensor_tensor(ve[:, which], mv[:, which, :, 1], ln_eps[:], ALU.add)
                g.tensor_tensor(neg_mean[:, which], mv[:, which, :, 0], minus_one[:], ALU.mult
                                ).then_inc(s[f"ve{which}_ready"], 1)
                pool.wait_ge(s[f"ve{which}_ready"], count)
                g.tensor_tensor(rstd[:, which], ve[:, which], neg_half[:], ALU.pow
                                ).then_inc(s[f"pow{which}_done"], 1)
                pool.wait_ge(s[f"pow{which}_done"], count)
                g.tensor_tensor(shift[:, which], neg_mean[:, which], rstd[:, which], ALU.mult
                                ).then_inc(s[f"ln{which}_rstd"], 1)

            pool.wait_ge(s["consts"], 3)
            inv_std(0, 1)
            g.iota(iota8[:], [[1, NE]], base=0, channel_multiplier=0, allow_small_or_imprecise_dtypes=True)
            g.iota(list_base[:], [[LIST, NE]], base=0, channel_multiplier=0,
                   allow_small_or_imprecise_dtypes=True)
            g.iota(dest[:], [[2 * STEP, NS], [1, 2], [2 * P, TILES]], base=0, channel_multiplier=2)
            g.iota(steps16[:], [[0, NE], [BLK, LIST // BLK - 1]], base=0, channel_multiplier=0,
                   allow_small_or_imprecise_dtypes=True)
            g.iota(bnum[:], [[1, NB], [0, NE]], base=0, channel_multiplier=0, allow_small_or_imprecise_dtypes=True)
            g.iota(b256[:], [[BLK, NB]], base=0, channel_multiplier=0,
                   allow_small_or_imprecise_dtypes=True).then_inc(s["consts"], 1)
            g.memset(pads[:], 0.0).then_inc(s["pads_ready"], 1)
            pool.wait_ge(s["pads_ready"], 1)
            g.iota(pads[:].bitcast(I32)[:, :, :, D:ROW], [[BLK, PADS], [P, 2], [0, 1]], base=PAIRS,
                   channel_multiplier=1).then_inc(s["pads_ready"], 1)

            def scatters(i, first, last):
                if first == 0:
                    pool.wait_ge(s["pos_ready"], i - 1)
                    pool.wait_ge(s["dest_ready"], i - 1)
                    pool.wait_ge(s["rows_ready"], i - 1)
                    alone(pool)
                for m in range(first, last):
                    g.indirect_dma_start(
                        out=lists, out_offset=bass.IndirectOffsetOnAxis(ap=pos[:, m:m + 1], axis=0),
                        in_=rows[:, m // TILES, m % TILES, :], in_offset=None).then_inc(s["scattered"], 16)

            def iteration(i, head, tail, nxt, routed):
                cuts = [0, 2, 4, 5, 2 * TILES] if tail and routed and not head else None
                if cuts:
                    scatters(i, cuts[0], cuts[1])
                if nxt:
                    inv_std(0, i + 2)
                if tail:
                    inv_std(1, i)
                    if cuts:
                        scatters(i, cuts[1], cuts[2])
                    pool.wait_ge(s["attn_ready"], i)
                    Xs = X[:, bass.ds(TILES * (i - 1), TILES), :]
                    g.tensor_tensor(Xs, Xs, attn[:], ALU.add).then_inc(s["x1_ready"], 1)
                    if cuts:
                        scatters(i, cuts[2], cuts[3])
                    inv_std(2, i)
                if head:
                    pool.wait_ge(s["kv_sum"], 4 * i + 1)
                    pool.wait_ge(s["qn_ready"], i + 1)
                    if from_on(i, 1):
                        pool.wait_ge(s["out_done"], i)
                    g.tensor_tensor(Z[:, 1], KV[:, 1], qn[:], ALU.mult).then_inc(s["z1_ready"], 1)
                if cuts:
                    scatters(i, cuts[3], cuts[4])
                elif routed:
                    scatters(i, 0, 2 * TILES)

            all_iterations(pool, iteration)

            def scatter_block(b, n, turn):
                pool.wait_ge(s["blk_yr"], b + 1)
                alone(pool)
                for c in range(2):
                    g.indirect_dma_start(
                        out=results,
                        out_offset=bass.IndirectOffsetOnAxis(ap=xb[n][:].bitcast(I32)[:, c, D:ROW], axis=0),
                        in_=yb[n][:, c, :], in_offset=None).then_inc(blk_scat[n], 16)

            over_blocks(pool, scatter_block)
            def residual(n):
                pool.wait_ge(s["fin_n"], n + 1)
                f = SH[:, TILES * n:TILES * (n + 1)]
                g.tensor_tensor(f, f, X[:, TILES * n:TILES * (n + 1)], ALU.add).then_inc(s["fin_done"], 1)

            for n in range(NS):
                m = n % 3
                pool.wait_ge(s["fin_mv"], n + 1)
                g.tensor_tensor(ve[:, m], mv[:, m, :, 1], ln_eps[:], ALU.add)
                g.tensor_tensor(neg_mean[:, m], mv[:, m, :, 0], minus_one[:], ALU.mult).then_inc(s["fin_ve"], 1)
                if n >= 3:
                    pool.wait_ge(s["fin_n"], n - 2)
                pool.wait_ge(s["fin_ve"], n + 1)
                g.tensor_tensor(rstd[:, m], ve[:, m], neg_half[:], ALU.pow).then_inc(s["fin_pow"], 1)
                pool.wait_ge(s["fin_pow"], n + 1)
                g.tensor_tensor(shift[:, m], neg_mean[:, m], rstd[:, m], ALU.mult).then_inc(s["fin_shift"], 1)
                if n:
                    residual(n - 1)
            residual(NS - 1)

        @block.scalar
        def _(act):
            a = nc.scalar

            act.dma_start(wqkv_raw[:], w_qkv).then_inc(s["w_first"], 16)
            act.dma_start(bqkv_raw[:], b_qkv.rearrange("(c p) -> c p", p=P)).then_inc(s["bias_in"], 16)
            act.dma_start(wout_sb[:], w_out).then_inc(s["w_first"], 16)
            act.wait_ge(s["consts"], 2)
            a.activation(warm[:], one8[:], ACT.Exp)

            def normal(which, dst, src, ready, count):
                act.wait_ge(s[f"ln{which}_rstd"], count)
                for j in range(TILES):
                    ins = a.activation(dst(j), src(j), ACT.Identity, bias=shift[:, which, j:j + 1],
                                       scale=rstd[:, which, j:j + 1])
                ins.then_inc(s[ready], 1)

            def ln0_apply(st, again):
                if again:
                    act.wait_ge(s["t0_done"], st)
                normal(0, lambda j: xn[:, j], lambda j: Xt(st, j), "xn_ready", st + 1)

            def rows_to_project(st, again):
                act.wait_ge(s["t0_done"], st + 1)
                if again:
                    act.wait_ge(s["v_mm"], st)
                a.activation(xn_t[:], bT[:], ACT.Copy).then_inc(s["xnt_ready"], 1)

            def qk_maps(st, again):
                act.wait_ge(s["q_mm"], st + 1)
                if again:
                    act.wait_ge(s["qk_ready"], st)
                a.activation(e_qk[:, 0], bA[:], ACT.Exp, bias=bq_scaled[:], scale=E ** -0.5)
                a.activation(r_qk[:, 0], bA[:], ACT.Relu, bias=bq_scaled[:],
                             scale=E ** -0.5).then_inc(s["q_read"], 1)
                act.wait_ge(s["k_mm"], st + 1)
                a.activation(e_qk[:, 1], bB[:], ACT.Exp, bias=bk_col[:])
                a.activation(r_qk[:, 1], bB[:], ACT.Relu, bias=bk_col[:]).then_inc(s["qk_read"], 1)

            def v_twice(st, again):
                act.wait_ge(s["v_mm"], st + 1)
                if again:
                    act.wait_ge(s["vt_done"], E * st)
                v = bA[:].rearrange("p (t d) -> p t d", t=TILES)
                a.activation(vdup[:, :, 0:D], v, ACT.Copy)
                a.activation(vdup[:, :, D:2 * D], v, ACT.Copy).then_inc(s["vdup_ready"], 1)

            ln0_apply(0, False)
            rows_to_project(0, False)
            act.wait_ge(s["setup_dve"], 3)
            qk_maps(0, False)
            v_twice(0, False)
            act.wait_ge(s["w_rest"], 48)
            a.activation(w1s_hi[:], w1s_sb[:], ACT.Copy).then_inc(s["w1s_hi"], 1)

            def gelus(st, first, last):
                for c in range(first, last):
                    act.wait_ge(s["fc_done"], CH * st + c + 1)
                    a.activation(hs[:, c], bH[:], ACT.Gelu_apprx_tanh,
                                 bias=bias_cols[:, NE * CH + c:NE * CH + c + 1]).then_inc(s["gelu_done"], 1)

            def shared_out(st):
                act.wait_ge(s["sh_done"], st + 1)
                a.activation(SH[:, bass.ds(TILES * st, TILES), :], bA[:].rearrange("p (t d) -> p t d", t=TILES),
                             ACT.Copy).then_inc(s["sh_read"], 1)

            def iteration(i, head, tail, nxt, routed):
                if head:
                    act.wait_ge(s["qk_ready"], i + 1)
                    if from_on(i, 1):
                        act.wait_ge(s["kc_ready"], i)
                    a.activation(k1[:], qk0[:, 1], ACT.Copy, bias=FEAT_EPS).then_inc(s["k1_ready"], 1)
                if routed:
                    if head:
                        gelus(i - 2, 0, 1)
                    act.wait_ge(s["xn2_ready"], i - 1)
                    if from_on(i, 3):
                        act.wait_ge(s["scattered"], 16 * 2 * TILES * (i - 2))
                    for k in range(2):
                        ins = a.activation(rows[:, k, :, 0:D], xn2[:], ACT.Copy)
                    ins.then_inc(s["rows_ready"], 1)
                if routed and not head and not tail:
                    act.wait_ge(s["idx_ready"], NS)
                    a.activation(gates[:, 1], gap[:], ACT.Exp).then_inc(s["gate_exp"], 1)
                    routed = False
                if routed:
                    gelus(i - 2, 1 if head else 0, 2)
                if nxt:
                    ln0_apply(i + 1, True)
                if routed and head:
                    gelus(i - 2, 2, 3)
                if tail:
                    if from_on(i, 2):
                        act.wait_ge(s["x1_ready"], i - 1)
                    normal(1, lambda j: attn[:, j], lambda j: bO[:, j * D:(j + 1) * D], "attn_ready", i)
                if nxt:
                    rows_to_project(i + 1, True)
                if routed:
                    gelus(i - 2, 3 if head else 2, 4)
                    shared_out(i - 2)
                if nxt:
                    qk_maps(i + 1, True)
                if nxt:
                    v_twice(i + 1, True)
                if tail:
                    if from_on(i, 2):
                        act.wait_ge(s["t2_done"], i - 1)
                    normal(2, lambda j: xn2[:, j], lambda j: Xt(i - 1, j), "xn2_ready", i)
                if tail:
                    act.wait_ge(s["t2_done"], i)
                    if from_on(i, 2):
                        act.wait_ge(s["fc_done"], CH * (i - 1))
                    a.activation(xt2_hi[:], bT[:], ACT.Copy)
                    a.activation(xt2[:], bT[:], ACT.Copy).then_inc(s["xt2_ready"], 1)

            all_iterations(act, iteration)

            def step(b, n, turn):
                if not isinstance(b, int) or b < NB:
                    act.wait_ge(wb_in[n], 16 * turn(0) + 16)
                    if from_on(b, 2):
                        act.wait_ge(s["blk_fc"], b - 1)
                    a.activation(w_hi[n % 2][:], wb[n][:, 0:HID], ACT.Copy).then_inc(s["blk_whi"], 1)
                if from_on(b, 1):
                    m = (n - 1) % NBUF
                    act.wait_ge(s["blk_fc"], b)
                    if from_on(b, 3):
                        act.wait_ge(s["blk_mm2"], b - 2)
                    for c in range(CH):
                        ins = a.activation(hb[m % 2][:, c],
                                           blk_h[m % 2][c // 2][:, (c % 2) * BLK:(c % 2 + 1) * BLK],
                                           ACT.Gelu_apprx_tanh, bias=wb[m][:, B1_AT + c:B1_AT + c + 1])
                    ins.then_inc(s["blk_gelu"], 1)

            over_blocks(act, step, extra=1)

            act.wait_ge(s["blk_mm2"], NB)
            gelus(NS - 1, 0, CH - 1)

            def second_gated(g):
                act.wait_ge(y_in[g], 16)
                for j in range(TILES):
                    n = TILES * g + j
                    y = Y[g // PER_Y][:, g % PER_Y, j, 1]
                    ins = a.activation(y, y, ACT.Copy, scale=gates[:, 1, n:n + 1])
                ins.then_inc(s["fin_scaled"], 1)

            AHEAD = 4
            act.wait_ge(s["gate_w"], 3)
            second_gated(0)
            gelus(NS - 1, CH - 1, CH)
            second_gated(1)
            shared_out(NS - 1)
            for g in range(2, AHEAD):
                second_gated(g)
            for n in range(NS):
                m = n % 3
                act.wait_ge(s["fin_shift"], n + 1)
                for j in range(TILES):
                    f = SH[:, TILES * n + j]
                    ins = a.activation(f, f, ACT.Identity, bias=shift[:, m, j:j + 1], scale=rstd[:, m, j:j + 1])
                ins.then_inc(s["fin_n"], 1)
                if n + AHEAD < NS:
                    second_gated(n + AHEAD)

        @block.tensor
        def _(pe):
            t = nc.tensor
            pe.wait_ge(s["consts"], 3)
            pe.wait_ge(s["bias_in"], 48)
            pe.wait_ge(s["setup_dve"], 1)
            t.transpose(bS[:, 0:NBIAS], bias_rows[:], ident[0:NBIAS, 0:NBIAS])
            t.transpose(bS[:, 64:67], bqkv_rows[:].rearrange("r e h -> r (e h)"), ident[0:3, 0:3]
                        ).then_inc(s["setup_pe"], 1)
            pe.wait_ge(s["w_first"], 32)
            t.transpose(bO[:, 0:D], wout_sb[:], ident[:]).then_inc(s["setup_pe"], 1)

            def transposes(src, done):
                for j in range(TILES):
                    ins = t.transpose(bT[:, j * P:(j + 1) * P], src[:, j], ident[:])
                ins.then_inc(s[done], 1)

            def add_bias(bank, which):
                t.matmul(bank[:].rearrange("p (t d) -> p t d", t=TILES), ones3[:],
                         bias3[:, which].unsqueeze(1).broadcast_to([P, TILES, D]), start=True, stop=False,
                         skip_group_check=True)

            def ln0_transposes(st):
                pe.wait_ge(s["xn_ready"], st + 1)
                if from_on(st, 3):
                    pe.wait_ge(s["xt2_ready"], st - 2)
                transposes(xn, "t0_done")

            def project(st, again):
                pe.wait_ge(s["xnt_ready"], st + 1)
                if from_on(st, 3):
                    pe.wait_ge(s["sh_read"], st - 2)
                t.matmul(bA[:], w3[:, 0:D], xn_t[:], start=True, stop=True).then_inc(s["q_mm"], 1)
                if again:
                    pe.wait_ge(s["qn_ready"], st)
                t.matmul(bB[:], w3[:, D:2 * D], xn_t[:], start=True, stop=True).then_inc(s["k_mm"], 1)
                pe.wait_ge(s["q_read"], st + 1)
                add_bias(bA, 0)
                for j in range(TILES):
                    ins = t.matmul(bA[:, j * D:(j + 1) * D], xn_t[:, j * P:(j + 1) * P], w3[:, 2 * D:3 * D],
                                   start=False, stop=True, skip_group_check=True)
                ins.then_inc(s["v_mm"], 1)

            pe.wait_ge(s["setup_dve"], 4)
            w2t = wout_t[:].rearrange("p a e h -> p (a e h)")
            for d in range(E):
                dst = bV[d // 4][:, (d % 4) * D:(d % 4 + 1) * D]
                ins = t.transpose(dst, w2t[:, d * H:d * H + D], ident[:])
            ins.then_inc(s["setup_pe"], 1)
            w3 = wqkv_sb[:].rearrange("p m e h -> p (m e h)")
            ln0_transposes(0)
            pe.wait_ge(s["bias_parts"], 7)
            project(0, False)
            pe.wait_ge(s["setup_dve"], 5)

            def v_rotated(st, d, again):
                if again or d >= 2:
                    pe.wait_ge(s["kv_prod"], E * st + d - 1)
                for j in range(TILES):
                    ins = t.transpose(bV[d % 2][:, j * P:(j + 1) * P], vdup[:, j, d * H:d * H + D], ident[:])
                ins.then_inc(s["vt_done"], 1)

            def first_v(st, again):
                pe.wait_ge(s["vdup_ready"], st + 1)
                v_rotated(st, 0, again)
                v_rotated(st, 1, again)

            def fc(st, c, again):
                if again or c >= 1:
                    pe.wait_ge(s["gelu_done"], CH * st + c)
                hi, lo = [part[:, c * P:(c + 1) * P] for part in (w1s_hi, w1s_lo)]
                t.matmul(bH[:], hi, xt2_lo[:], start=True, stop=False)
                t.matmul(bH[:], hi, xt2_hi[:], start=False, stop=False)
                t.matmul(bH[:], lo, xt2_hi[:], start=False, stop=True).then_inc(s["fc_done"], 1)

            def proj(st, c):
                pe.wait_ge(s["gelu_done"], CH * st + c + 1)
                for j in range(TILES):
                    ins = t.matmul(bA[:, j * D:(j + 1) * D], hs[:, c, j * P:(j + 1) * P], w2s_sb[:, c],
                                   start=False, stop=True, skip_group_check=True)
                if c == CH - 1:
                    ins.then_inc(s["sh_done"], 1)

            def proj_bias(st):
                if from_on(st, 1):
                    pe.wait_ge(s["sh_read"], st)
                add_bias(bA, 2)

            def out_part(st, part):
                pe.wait_ge(s["z_ready"], 4 * st + part + 1)
                if part == 1:
                    pe.wait_ge(s["z1_ready"], st + 1)
                for d in ((0,), (1, 2, 3), (4, 5), (6, 7))[part]:
                    for j in range(TILES):
                        ins = t.matmul(bO[:, j * D:(j + 1) * D], Z[:, d, j * P:(j + 1) * P], wout_rot[:, d],
                                       start=False, stop=True, skip_group_check=True)
                if part == 3:
                    ins.then_inc(s["out_done"], 1)

            def logits(i):
                if from_on(i, 3):
                    pe.wait_ge(s["acc_ready"], i - 2)
                for j in range(TILES):
                    ins = t.matmul(ps_lg[:, j * NE:(j + 1) * NE], xt2[:, j * P:(j + 1) * P], wr_sb[:],
                                   start=True, stop=True)
                ins.then_inc(s["lg_done"], 1)

            def ranks(i):
                pe.wait_ge(s["chosen_ready"], i - 1)
                rk = ps_rank.rearrange("p (t e) -> p t e", t=TILES)
                t.matmul(ps_rank, before[:], chosen[:].rearrange("p t e -> p (t e)"), start=True,
                         stop=False, skip_group_check=True)
                for j in range(TILES - 1):
                    n = TILES - 1 - j
                    t.matmul(rk[:, j + 1:, :], ones_bf[:],
                             chosen[:, j, :].unsqueeze(1).broadcast_to([P, n, NE]), start=False, stop=False,
                             skip_group_check=True)
                t.matmul(rk, ones_bf[:], chosen_acc[:].unsqueeze(1).broadcast_to([P, TILES, NE]), start=False,
                         stop=True, skip_group_check=True).then_inc(s["rank_done"], 1)

            def iteration(i, head, tail, nxt, routed):
                again = from_on(i, 1)
                ga = from_on(i, 3)
                if isinstance(i, int) and i == 2:
                    pe.wait_ge(s["w1s_lo"], 1)
                if head:
                    v_rotated(i, 2, again)
                    v_rotated(i, 3, again)
                if routed:
                    pe.wait_ge(s["xt2_ready"], i - 1)
                    if not head and not tail:
                        logits(i)
                        ranks(i)
                    if not head:
                        pe.wait_ge(s["acc_ready"], i - 1)
                        t.matmul(bS[:, 0:NE], ones_bf[:], chosen_acc[:], start=True, stop=True
                                 ).then_inc(s["cnt_done"], 1)
                    if not head and not tail:
                        return
                    proj_bias(i - 2)
                    pe.wait_ge(s["xt2_lo"], i - 1)
                    fc(i - 2, 0, ga)
                    if head:
                        logits(i)
                    fc(i - 2, 1, ga)
                    proj(i - 2, 0)
                if head:
                    pe.wait_ge(s["qk_read"], i + 1)
                    pe.wait_ge(s["p_ready"], i + 1)
                    for j in range(TILES):
                        ins = t.matmul(ps_den[:, j * H:(j + 1) * H], pden[:, j * P:(j + 1) * P], head_ones[:],
                                       start=True, stop=True)
                    ins.then_inc(s["den_done"], 1)
                    v_rotated(i, 4, again)
                if routed:
                    fc(i - 2, 2, ga)
                if head:
                    v_rotated(i, 5, again)
                if routed:
                    proj(i - 2, 1)
                if nxt:
                    ln0_transposes(i + 1)
                if routed:
                    fc(i - 2, 3, ga)
                    proj(i - 2, 2)
                    if head:
                        ranks(i)
                    proj(i - 2, 3)
                if head:
                    pe.wait_ge(s["rden_ready"], i + 1)
                    for j in range(TILES):
                        ins = t.transpose(bB[:, j * P:(j + 1) * P],
                                          rden8[:, j].rearrange("p e h -> p (e h)"), ident[:])
                    ins.then_inc(s["exp_done"], 1)
                    v_rotated(i, 6, again)
                    v_rotated(i, 7, again)
                if nxt:
                    project(i + 1, True)
                if head:
                    if again:
                        pe.wait_ge(s["attn_ready"], i)
                    add_bias(bO, 1)
                    out_part(i, 0)
                if nxt:
                    first_v(i + 1, True)
                if head and nxt:
                    out_part(i, 1)
                if tail:
                    if nxt:
                        pe.wait_ge(s["xnt_ready"], i + 2)
                    pe.wait_ge(s["xn2_ready"], i)
                    transposes(xn2, "t2_done")
                if head and not nxt:
                    out_part(i, 1)
                if head and not nxt:
                    pe.wait_ge(s["xt2_ready"], i)
                    logits(i + 1)
                if head:
                    out_part(i, 2)
                if head and not nxt:
                    ranks(i + 1)
                if head:
                    out_part(i, 3)

            pe.wait_ge(s["w_rest"], 48)
            first_v(0, False)
            all_iterations(pe, iteration)
            pe.wait_ge(s["cnt_read"], 2)
            pe.wait_ge(s["sh_read"], NS - 1)

            def step(b, n, turn):
                if not isinstance(b, int) or b < NB:
                    pe.wait_ge(xb_in[n], 16 * turn(0) + 16)
                    if from_on(b, 2):
                        pe.wait_ge(s["blk_tr"], b - 1)
                    for c in range(2):
                        ins = t.transpose(blk_t[n % 2][:, c * P:(c + 1) * P], xb[n][:, c, 0:D], ident[:])
                    ins.then_inc(s["blk_tp"], 1)
                if from_on(b, 1) and (not isinstance(b, int) or b - 1 < NB):
                    m = (n - 1) % NBUF
                    pe.wait_ge(wb_in[m], 16 * turn(1) + 16)
                    pe.wait_ge(s["blk_tr"], b)
                    if from_on(b, 3):
                        pe.wait_ge(s["blk_gelu"], b - 2)
                    pe.wait_ge(s["blk_wlo"], b)
                    for c in range(CH):
                        w = [part[m % 2][:, c * P:(c + 1) * P] for part in (w_hi, w_lo)]
                        h = blk_h[m % 2][c // 2][:, (c % 2) * BLK:(c % 2 + 1) * BLK]
                        t.matmul(h, w[0], x_lo[m % 2][:], start=True, stop=False)
                        t.matmul(h, w[0], x_hi[m % 2][:], start=False, stop=False)
                        ins = t.matmul(h, w[1], x_hi[m % 2][:], start=False, stop=True)
                    ins.then_inc(s["blk_fc"], 1)
                if from_on(b, 2):
                    m = (n - 2) % NBUF
                    pe.wait_ge(s["blk_gelu"], b - 1)
                    if from_on(b, 4):
                        pe.wait_ge(s["blk_yr"], b - 3)
                    for c in range(CH):
                        for r in range(2):
                            ins = t.matmul(blk_y[m % 2][:, r * D:(r + 1) * D], hb[m % 2][:, c, r * P:(r + 1) * P],
                                           wb[m][:, HID + c * D:HID + (c + 1) * D],
                                           start=(c == 0 and r == 0), stop=True, skip_group_check=True)
                    ins.then_inc(s["blk_mm2"], 1)

            over_blocks(pe, step, extra=2)
            pe.wait_ge(s["blk_tr"], NB)
            proj_bias(NS - 1)
            for c in range(CH):
                if c:
                    pe.wait_ge(s["gelu_done"], CH * (NS - 1) + c)
                t.matmul(bH[:], w1s_sb[:, c * P:(c + 1) * P], xt2[:], start=True, stop=True
                         ).then_inc(s["fc_done"], 1)
                proj(NS - 1, c)

        @block.vector
        def _(dve):
            v = nc.vector
            def sums_of(which, src):
                for j in range(TILES):
                    ins = v.bn_stats(bst[:, which, j], src(j))
                ins.then_inc(s[f"ln{which}_st"], 1)

            def mean_var(which, count):
                dve.wait_ge(s[f"ln{which}_st"], count)
                alone(dve)
                for j in range(TILES):
                    ins = v.bn_aggr(mv[:, which, j], bst[:, which, j])
                ins.then_inc(s[f"ln{which}_mv"], 1)

            def ln0_sums(st):
                sums_of(0, lambda j: Xt(st, j))

            dve.wait_ge(s["x_first"], 16)
            ln0_sums(0)
            mean_var(0, 1)
            dve.wait_ge(s["consts"], 3)
            dve.wait_ge(s["bias_in"], 48)
            v.tensor_copy(bqkv_rows[:], bqkv_raw[:].rearrange("r (h e) -> r e h", h=H)
                          ).then_inc(s["setup_dve"], 1)
            v.tensor_reduce(head_ones[:], ident[:].rearrange("p (e h) -> p h e", e=E), AX_X, ALU.add)
            dve.wait_ge(s["w_first"], 32)
            for m in range(3):
                ins = v.tensor_copy(wqkv_sb[:, m], wqkv_raw[:, m * D:(m + 1) * D].rearrange("p (h e) -> p e h", h=H))
            ins.then_inc(s["setup_dve"], 1)
            dve.wait_ge(s["setup_pe"], 1)
            v.tensor_copy(bias_cols[:], bS[:, 0:NBIAS])
            v.tensor_copy(bk_col[:], bS[:, 65:66])
            v.tensor_scalar(bq_scaled[:], bS[:, 64:65], E ** -0.5, None, ALU.mult).then_inc(s["setup_dve"], 1)
            dve.wait_ge(s["setup_dve"], 3)
            v.tensor_copy(b12[:, :, 0:CH], bias_cols[:, 0:NE * CH].rearrange("p (e c) -> p e c", e=NE))
            dve.wait_ge(s["setup_pe"], 2)
            for half in range(2):
                ins = v.tensor_copy(wout_t[:, half], bO[:, 0:D].rearrange("p (h e) -> p e h", h=H))
            ins.then_inc(s["setup_dve"], 1)

            dve.wait_ge(s["rows_in"], 48)
            v.tensor_copy(bias_f[:, 0].rearrange("p (e h) -> p e h", e=E),
                          bias_raw[:, 0].rearrange("p (h e) -> p e h", h=H))
            v.tensor_copy(bias_f[:, 1:3], bias_raw[:, 1:3]).then_inc(s["bias_parts"], 1)
            for n in range(3):
                v.memset(ones3[32 * n:32 * n + 1, :], 1.0)
                dve.wait_ge(s["bias_parts"], 2 * n + 1)
                v.tensor_copy(bias_part[n][:], bias_f[:]).then_inc(s["bias_parts"], 1)
                dve.wait_ge(s["bias_parts"], 2 * n + 2)
                ins = v.tensor_copy(bias3[32 * n:32 * n + 1], bias_part[n][32 * n:32 * n + 1])
                if n < 2:
                    ins = v.tensor_tensor(bias_f[:], bias_f[:], bias_part[n][:], ALU.subtract)
                ins.then_inc(s["bias_parts"], 1)

            dve.wait_ge(s["setup_pe"], 3)
            for half in range(2):
                ins = v.tensor_copy(wout_rot[:, 4 * half:4 * half + 4],
                                    bV[half][:].rearrange("p (a d) -> p a d", a=4))
            ins.then_inc(s["setup_dve"], 1)
            dve.wait_ge(s["x_second"], 16)

            def prod(i, d):
                if d == 1 and from_on(i, 1):
                    dve.wait_ge(s["z1_ready"], i)
                dve.wait_ge(s["vt_done"], E * i + d + 1)
                v.scalar_tensor_tensor(out=KV[:, d], in0=qk0[:, 1], scalar=FEAT_EPS, in1=bV[d % 2][:],
                                       op0=ALU.add, op1=ALU.mult).then_inc(s["kv_prod"], 1)

            def sums(i, part):
                dve.wait_ge(s["kv_prod"], E * i + 2 * part + 2)
                w = KV[:, 2 * part:2 * part + 2].rearrange("p a t -> p (a t)")
                v.tensor_tensor_scan(w, keep[:], w, 0.0, ALU.mult, ALU.add).then_inc(s["kv_sum"], 1)

            def zed(i, part):
                dve.wait_ge(s["kv_sum"], 4 * i + part + 1)
                if part == 0:
                    v.tensor_tensor(Z[:, 0], KV[:, 0], qn[:], ALU.mult).then_inc(s["z_ready"], 1)
                    return
                v.tensor_tensor(Z[:, 2 * part:2 * part + 2], KV[:, 2 * part:2 * part + 2],
                                qn[:].unsqueeze(1).broadcast_to([P, 2, STEP]), ALU.mult).then_inc(s["z_ready"], 1)

            def logits_in(i):
                dve.wait_ge(s["lg_done"], i - 1)
                v.tensor_copy(lg[:], ps_lg.rearrange("p (t e) -> p t e", t=TILES)).then_inc(s["lg_read"], 1)

            def route_top(i):
                dve.wait_ge(s["lg_read"], i - 1)
                alone(dve)
                for j in range(TILES):
                    v.max(top[:, j], lg[:, j]).then_inc(s["top_ready"], 1)
                dve.wait_ge(s["top_ready"], 2 * TILES * (i - 2) + TILES)
                alone(dve)
                for j in range(TILES):
                    v.max_index(topi[:, j], top[:, j], lg[:, j]).then_inc(s["top_ready"], 1)
                g = gap[:, bass.ds(TILES * (i - 2), TILES)]
                v.tensor_tensor(g, top[:, :, 1], top[:, :, 0], ALU.subtract)
                dve.wait_ge(s["top_ready"], 2 * TILES * (i - 1))
                v.tensor_copy(idxf[:], topi[:, :, 0:2].rearrange("p t k -> p k t")
                              ).then_inc(s["idx_ready"], 1)

            def route_hot(i):
                dve.wait_ge(s["idx_ready"], i - 1)
                v.tensor_tensor(onehot[:].rearrange("p k t e -> p (k t) e"),
                                idxf[:].rearrange("p k t -> p (k t)").unsqueeze(2)
                                .broadcast_to([P, 2 * TILES, NE]),
                                iota8[:].unsqueeze(1).broadcast_to([P, 2 * TILES, NE]),
                                ALU.is_equal).then_inc(s["hot_ready"], 1)

            def route_chosen(i):
                dve.wait_ge(s["hot_ready"], i - 1)
                if from_on(i, 3):
                    dve.wait_ge(s["rank_done"], i - 2)
                v.tensor_tensor(chosen[:], onehot[:, 0], onehot[:, 1], ALU.add).then_inc(s["chosen_ready"], 1)

            def route_sum(i):
                dve.wait_ge(s["chosen_ready"], i - 1)
                v.tensor_reduce(chosen_sum[:], chosen[:].rearrange("p t e -> p e t"), AX_X,
                                ALU.add).then_inc(s["acc_red"], 1)

            def route_place(i):
                dve.wait_ge(s["rank_done"], i - 1)
                v.tensor_tensor(place[:], ps_rank.rearrange("p (t e) -> p t e", t=TILES),
                                list_base[:].unsqueeze(1).broadcast_to([P, TILES, NE]),
                                ALU.add).then_inc(s["place_ready"], 1)
                dve.wait_ge(s["acc_red"], i - 1)
                v.tensor_tensor(chosen_acc[:], chosen_acc[:], chosen_sum[:], ALU.add
                                ).then_inc(s["acc_ready"], 1)
                dve.wait_ge(s["place_ready"], i - 1)
                v.tensor_tensor(placed[:], onehot[:], place[:].unsqueeze(1).broadcast_to([P, 2, TILES, NE]),
                                ALU.mult).then_inc(s["placed_ready"], 1)

            def route_pos(i):
                dve.wait_ge(s["placed_ready"], i - 1)
                v.tensor_reduce(posf[:], placed[:].rearrange("p k t e -> p (k t) e"), AX_X,
                                ALU.add).then_inc(s["posf_ready"], 1)
                if from_on(i, 3):
                    dve.wait_ge(s["scattered"], 16 * 2 * TILES * (i - 2))
                dst = dest[:, i - 2] if isinstance(i, int) else \
                    dest[:, bass.ds(i - 2, 1)].rearrange("p o k t -> p (o k) t")
                v.tensor_copy(rows[:].bitcast(I32)[:, :, :, D:ROW].rearrange("p k t o -> p k (t o)"),
                              dst).then_inc(s["dest_ready"], 1)
                dve.wait_ge(s["posf_ready"], i - 1)
                v.tensor_copy(pos[:], posf[:]).then_inc(s["pos_ready"], 1)

            def route(i):
                for part in (logits_in, route_top, route_hot, route_chosen, route_sum, route_place, route_pos):
                    part(i)

            def low_part(i):
                dve.wait_ge(s["xt2_ready"], i - 1)
                if from_on(i, 3):
                    dve.wait_ge(s["fc_done"], CH * (i - 2))
                v.tensor_tensor(xt2_lo[:], xt2[:], xt2_hi[:].bitcast(F32), ALU.subtract
                                ).then_inc(s["xt2_lo"], 1)

            links = [0]

            def link(ins):
                links[0] += 1
                ins.then_inc(s["tab"], 1)
                dve.wait_ge(s["tab"], links[0])

            M = LIST // BLK - 1

            def list_blocks(counts, compare):
                link(v.tensor_tensor(full16[:], counts.unsqueeze(2).broadcast_to([1, NE, M]), steps16[:], compare))
                link(v.tensor_reduce(nblk[:], full16[:], AX_X, ALU.add))

            def block_experts(first, last, ends_of):
                k = last - first
                link(v.tensor_tensor(past[:, 0:k], bnum[:, 0:k], ends_of.unsqueeze(1).broadcast_to([1, k, NE]),
                                     ALU.is_ge))
                link(v.tensor_reduce(tabf[:, first:last], past[:, 0:k], AX_X, ALU.add))
                link(v.tensor_scalar(tabf[:, first:last], tabf[:, first:last], float(NE - 1), None, ALU.min))

            def block_rows(first, last):
                k, at = last - first, tabf[:, NB + first:NB + last]
                link(v.tensor_tensor(pastj[:, 0:k], past[:, 0:k], jump[:].unsqueeze(1).broadcast_to([1, k, NE]),
                                     ALU.mult))
                link(v.tensor_reduce(at, pastj[:, 0:k], AX_X, ALU.add))
                link(v.scalar_tensor_tensor(out=at, in0=at, scalar=first_row[:], in1=b256[:, 0:k], op0=ALU.add,
                                            op1=ALU.add))
                v.tensor_copy(table[:, first:last], tabf[:, first:last])
                v.tensor_copy(table[:, NB + first:NB + last], at).then_inc(s["table_ready"], 1)

            def early_table():
                dve.wait_ge(s["cnt_done"], 1)
                v.tensor_copy(cnt[:], bS[0:1, 0:NE]).then_inc(s["cnt_read"], 1)
                dve.wait_ge(s["cnt_read"], 1)
                link(v.tensor_scalar(cnt[:], cnt[:], -float(BLK), None, ALU.add))
                list_blocks(cnt[:], ALU.is_ge)
                link(v.tensor_tensor_scan(cum[:], one8[:], nblk[:], 0.0, ALU.mult, ALU.add))
                link(v.tensor_scalar(cum_done[:, 1:], cum[:], float(EARLY), None, ALU.min))
                v.tensor_scalar(first_row[:], one8[:, 0:1], 0.0, None, ALU.mult)
                link(v.tensor_tensor(done[:, 0:NE], cum_done[:, 1:], cum_done[:, 0:NE], ALU.subtract))
                link(v.tensor_scalar(jump[:], done[:, 0:NE], -float(BLK), float(LIST), ALU.mult, ALU.add))
                block_experts(0, EARLY, cum_done[:, 1:])
                block_rows(0, EARLY)

            def late_table(part):
                if part == 1:
                    list_blocks(cnt[:], ALU.is_gt)
                    link(v.tensor_tensor(nblk[:], nblk[:], done[:, 0:NE], ALU.subtract))
                if part == 2:
                    v.tensor_tensor(step_up[:], done[:, 1:], done[:, 0:NE], ALU.subtract)
                    v.tensor_scalar(first_row[:], done[:, 0:1], float(BLK), None, ALU.mult)
                    link(v.tensor_tensor_scan(cum[:], one8[:], nblk[:], 0.0, ALU.mult, ALU.add))
                    link(v.tensor_tensor(step_up[:], step_up[:], nblk[:], ALU.subtract))
                    link(v.tensor_scalar(jump[:], step_up[:], float(BLK), float(LIST), ALU.mult, ALU.add))
                if part == 3:
                    block_experts(EARLY, NB, cum[:])
                if part == 4:
                    block_rows(EARLY, NB)

            def iteration(i, head, tail, nxt, routed):
                again = from_on(i, 1)
                if isinstance(i, int) and i == 1:
                    dve.wait_ge(s["w1s_hi"], 1)
                    v.tensor_tensor(w1s_lo[:], w1s_sb[:], w1s_hi[:].bitcast(F32), ALU.subtract
                                    ).then_inc(s["w1s_lo"], 1)
                if not head:
                    route(i)
                    routed = False
                    if tail:
                        low_part(i)
                if head:
                    dve.wait_ge(s["qk_read"], i + 1)
                    if again:
                        dve.wait_ge(s["k1_ready"], i)
                    v.scalar_tensor_tensor(out=qk0[:], in0=e_qk[:], scalar=1.0, in1=r_qk[:], op0=ALU.min,
                                           op1=ALU.add).then_inc(s["qk_ready"], 1)
                if nxt:
                    if isinstance(i, int) and i == 1:
                        dve.wait_ge(s["x_rest"], 16)
                    ln0_sums(i + 1)
                if head:
                    dve.wait_ge(s["qk_ready"], i + 1)
                    prod(i, 0)
                    prod(i, 1)
                if routed:
                    low_part(i)
                if nxt:
                    mean_var(0, i + 2)
                if head:
                    dve.wait_ge(s["k1_ready"], i + 1)
                    v.tensor_tensor_scan(KC[:], keep[:, 0:STEP], k1[:], 0.0, ALU.mult,
                                         ALU.add).then_inc(s["kc_ready"], 1)
                    dve.wait_ge(s["kc_ready"], i + 1)
                    if again:
                        dve.wait_ge(s["den_done"], i)
                    v.scalar_tensor_tensor(out=pden[:], in0=qk0[:, 0], scalar=FEAT_EPS, in1=KC[:], op0=ALU.add,
                                           op1=ALU.mult).then_inc(s["p_ready"], 1)
                    prod(i, 2)
                    prod(i, 3)
                if tail:
                    dve.wait_ge(s["out_done"], i)
                    sums_of(1, lambda j: bO[:, j * D:(j + 1) * D])
                if routed:
                    logits_in(i)
                if tail:
                    mean_var(1, i)
                if tail and not head:
                    early_table()
                if routed:
                    route_top(i)
                if head:
                    sums(i, 0)
                if routed:
                    route_hot(i)
                if head:
                    dve.wait_ge(s["den_done"], i + 1)
                    v.tensor_scalar(den[:], ps_den, DEN_EPS, None, ALU.add).then_inc(s["den_add"], 1)
                    prod(i, 4)
                if routed:
                    route_chosen(i)
                if head:
                    dve.wait_ge(s["den_add"], i + 1)
                    v.reciprocal(rden[:].rearrange("p t h -> p (t h)"), den[:]).then_inc(s["den_inv"], 1)
                    prod(i, 5)
                    dve.wait_ge(s["den_inv"], i + 1)
                    if again:
                        dve.wait_ge(s["exp_done"], i)
                    v.tensor_copy(rden8[:], rden[:].unsqueeze(2).broadcast_to([P, TILES, E, H])
                                  ).then_inc(s["rden_ready"], 1)
                if head:
                    sums(i, 1)
                if routed:
                    route_sum(i)
                if tail:
                    dve.wait_ge(s["x1_ready"], i)
                    sums_of(2, lambda j: Xt(i - 1, j))
                if routed:
                    route_place(i)
                if tail:
                    mean_var(2, i)
                if head:
                    prod(i, 6)
                    dve.wait_ge(s["exp_done"], i + 1)
                    v.scalar_tensor_tensor(out=qn[:], in0=qk0[:, 0], scalar=FEAT_EPS, in1=bB[:], op0=ALU.add,
                                           op1=ALU.mult).then_inc(s["qn_ready"], 1)
                    prod(i, 7)
                if routed:
                    route_pos(i)
                if head:
                    dve.wait_ge(s["qn_ready"], i + 1)
                    if again:
                        dve.wait_ge(s["out_done"], i)
                    zed(i, 0)
                    sums(i, 2)
                    zed(i, 1)
                    sums(i, 3)
                    zed(i, 2)
                    zed(i, 3)

            dve.wait_ge(s["consts"], 4)
            all_iterations(dve, iteration)

            dve.wait_ge(s["cnt_done"], 2)
            v.tensor_copy(cnt[:], bS[0:1, 0:NE]).then_inc(s["cnt_read"], 1)
            dve.wait_ge(s["cnt_read"], 2)
            link(v.tensor_tensor(tabf[:, 2 * NB:2 * NB + NE], cnt[:], list_base[0:1, :], ALU.add))
            v.tensor_copy(ends[:], tabf[:, 2 * NB:2 * NB + NE]).then_inc(s["ends_ready"], 1)

            def step(b, n, turn):
                if not isinstance(b, int) or b < NB:
                    dve.wait_ge(s["blk_tp"], b + 1)
                    if from_on(b, 2):
                        dve.wait_ge(s["blk_fc"], b - 1)
                    v.tensor_copy(x_hi[n % 2][:], blk_t[n % 2]).then_inc(s["blk_xhi"], 1)
                    dve.wait_ge(s["blk_whi"], b + 1)
                    v.tensor_tensor(w_lo[n % 2][:], wb[n][:, 0:HID], w_hi[n % 2][:].bitcast(F32), ALU.subtract
                                    ).then_inc(s["blk_wlo"], 1)
                    dve.wait_ge(s["blk_xhi"], b + 1)
                    v.tensor_tensor(x_lo[n % 2][:], blk_t[n % 2], x_hi[n % 2][:].bitcast(F32), ALU.subtract
                                    ).then_inc(s["blk_tr"], 1)
                if from_on(b, 2):
                    m = (n - 2) % NBUF
                    dve.wait_ge(s["blk_mm2"], b - 1)
                    if from_on(b, NBUF + 2):
                        dve.wait_ge(blk_scat[m], 32 * turn(2))
                    v.tensor_tensor(yb[m][:], blk_y[m % 2][:, 0:2 * D].rearrange("p (r d) -> p r d", r=2),
                                    wb[m][:, B2_AT:WROW].unsqueeze(1).broadcast_to([P, 2, D]),
                                    ALU.add).then_inc(s["blk_yr"], 1)
                if isinstance(b, int) and 1 <= b <= 4:
                    late_table(b)

            over_blocks(dve, step, extra=2)

            dve.wait_ge(s["gate_exp"], 1)
            v.tensor_scalar(gates[:, 0], gates[:, 1], 1.0, None, ALU.add).then_inc(s["gate_w"], 1)
            dve.wait_ge(s["gate_w"], 1)
            v.reciprocal(gates[:, 0], gates[:, 0]).then_inc(s["gate_w"], 1)
            dve.wait_ge(s["gate_w"], 2)
            v.tensor_tensor(gates[:, 1], gates[:, 1], gates[:, 0], ALU.mult).then_inc(s["gate_w"], 1)
            dve.wait_ge(s["gate_w"], 3)

            def gated(g, k):
                if k == 0:
                    dve.wait_ge(y_in[g], 16)
                    for j in range(TILES):
                        n = TILES * g + j
                        ins = v.scalar_tensor_tensor(out=SH[:, n], in0=Y[g // PER_Y][:, g % PER_Y, j, 0],
                                                     scalar=gates[:, 0, n:n + 1], in1=SH[:, n], op0=ALU.mult,
                                                     op1=ALU.add)
                    ins.then_inc(s["fin_y0"], 1)
                else:
                    dve.wait_ge(s["fin_y0"], g + 1)
                    dve.wait_ge(s["fin_scaled"], g + 1)
                    f = SH[:, TILES * g:TILES * (g + 1)]
                    v.tensor_tensor(f, f, Y[g // PER_Y][:, g % PER_Y, :, 1], ALU.add).then_inc(s["fin_y1"], 1)

            def final_stats(g):
                dve.wait_ge(s["fin_y1"], g + 1)
                for j in range(TILES):
                    ins = v.bn_stats(bst[:, g % 3, j], SH[:, TILES * g + j])
                ins.then_inc(s["fin_st"], 1)

            def final_mean(g):
                dve.wait_ge(s["fin_st"], g + 1)
                if g >= 3:
                    dve.wait_ge(s["fin_shift"], g - 2)
                for j in range(TILES):
                    ins = v.bn_aggr(mv[:, g % 3, j], bst[:, g % 3, j])
                ins.then_inc(s["fin_mv"], 1)

            gated(0, 0)
            for g in range(NS + 1):
                if g + 1 == NS - 1:
                    dve.wait_ge(s["sh_read"], NS)
                if g + 1 < NS:
                    gated(g + 1, 0)
                if g:
                    final_stats(g - 1)
                if g < NS:
                    gated(g, 1)
                if g:
                    final_mean(g - 1)



_INS = ['L0_attn_x', 'L0_attn_W_qkv', 'L0_attn_b_qkv', 'L0_attn_W_out', 'L0_attn_b_out', 'L0_ffn_Wfc_s',
        'L0_ffn_bfc_s', 'L0_ffn_Wproj_s', 'L0_ffn_bproj_s', 'L0_ffn_Wr', 'L0_ffn_Wfc', 'L0_ffn_bfc',
        'L0_ffn_Wproj', 'L0_ffn_bproj']


def kernel(**inputs):
    import numpy as _np
    import concourse.bacc as _bacc
    from concourse import mybir as _mybir
    from concourse.bass_utils import run_bass_kernel_spmd as _run

    nc = _bacc.Bacc("TRN2", target_bir_lowering=False, num_devices=1)
    arrays, args = {}, []
    for name in _INS:
        a = _np.ascontiguousarray(inputs[name])
        arrays[f"in_{name}"] = a
        args.append(nc.dram_tensor(f"in_{name}", a.shape, _mybir.dt.from_np(a.dtype), kind="ExternalInput").ap())
    shape = inputs['L0_attn_x'].shape
    args.append(nc.dram_tensor("out_0", shape, _mybir.dt.float32, kind="ExternalOutput").ap())
    sandwich_kernel(nc, *args)
    r = _run(nc, [arrays], core_ids=[0])
    return r.results[0]["out_0"]
```
